# Optimizing a Trainium2 kernel written in Bass

```python
import numpy as np
import jax
import jax.numpy as jnp

def _softmax(x, axis=-1):
    return jax.nn.softmax(x, axis=axis)

def _gelu(x):
    return jax.nn.gelu(x, approximate=True)

def _silu(x):
    return jax.nn.silu(x)

def _sigmoid(x):
    return jax.nn.sigmoid(x)

def _layernorm(x, axis=-1, eps=1e-05):
    m = jnp.mean(x, axis=axis, keepdims=True)
    v = jnp.var(x, axis=axis, keepdims=True)
    return (x - m) / jnp.sqrt(v + eps)

def _scatter_add(tgt, idx, src, axis=0):
    return tgt.at[idx].add(src)

def _segment_sum(src, seg, n):
    return jax.ops.segment_sum(src, seg, n)
kernel_name = 'mk_adaln_d1_jaxref_r8_9ca452'

def setup_inputs(seed: int=0):
    np.random.seed(seed)
    _w = jnp.asarray

    def _L0_attn_setup():
        import jax, jax.numpy as jnp
        import numpy as np
        B, T, C, H = (2, 256, 128, 16)
        D_K = C // H
        key = jax.random.key(seed)
        kx, kq, kk, kv, ko = jax.random.split(key, 5)
        std_qkv = (2.0 / (C + H * D_K)) ** 0.5
        std_o = (2.0 / (H * D_K + C)) ** 0.5
        return {'x': jax.random.normal(kx, (B, T, C), dtype=jnp.float32), 'Q': jax.random.normal(kq, (C, H, D_K), dtype=jnp.float32) * std_qkv, 'K': jax.random.normal(kk, (C, H, D_K), dtype=jnp.float32) * std_qkv, 'V': jax.random.normal(kv, (C, H, D_K), dtype=jnp.float32) * std_qkv, 'O': jax.random.normal(ko, (H * D_K, C), dtype=jnp.float32) * std_o}
    _L0_attn_in = _L0_attn_setup()

    def _L0_ffn_setup():
        import jax, jax.numpy as jnp
        import numpy as np
        E = 8
        K = 2
        CAP_FACTOR = 1.0
        key = jax.random.key(seed)
        ks = jax.random.split(key, 5)
        B, T, C, H = (4, 256, 128, 512)
        x = jax.random.normal(ks[0], (B, T, C), dtype=jnp.float32)
        Wr = jax.random.normal(ks[1], (C, E), dtype=jnp.float32) * 0.02
        br = jnp.zeros((E,), jnp.float32)
        W1 = jax.random.normal(ks[2], (E, C, H), dtype=jnp.float32) * 0.02
        b1 = jnp.zeros((E, H), jnp.float32)
        W2 = jax.random.normal(ks[3], (E, H, C), dtype=jnp.float32) * 0.02
        b2 = jnp.zeros((E, C), jnp.float32)
        return {'x': x, 'Wr': Wr, 'br': br, 'W1': W1, 'b1': b1, 'W2': W2, 'b2': b2}
    _L0_ffn_in = _L0_ffn_setup()
    _L0_c = _w((lambda *s: np.random.randn(*s).astype(np.float32) * 0.05)(8, 128))
    _L0_wmod = _w((lambda *s: np.random.randn(*s).astype(np.float32) * 0.05)(128, 6 * 128) * 128 ** (-0.5))
    _d = {'L0_attn_x': _L0_attn_in['x'], 'L0_attn_Q': _L0_attn_in['Q'], 'L0_attn_K': _L0_attn_in['K'], 'L0_attn_V': _L0_attn_in['V'], 'L0_attn_O': _L0_attn_in['O'], 'L0_ffn_Wr': _L0_ffn_in['Wr'], 'L0_ffn_br': _L0_ffn_in['br'], 'L0_ffn_W1': _L0_ffn_in['W1'], 'L0_ffn_b1': _L0_ffn_in['b1'], 'L0_ffn_W2': _L0_ffn_in['W2'], 'L0_ffn_b2': _L0_ffn_in['b2'], 'L0_c': _L0_c, 'L0_wmod': _L0_wmod}
    _x0 = _d['L0_attn_x']
    _d['L0_attn_x'] = jax.random.normal(jax.random.fold_in(jax.random.key(seed), 1), (8, 512, 128), dtype=_x0.dtype)
    del _x0
    return _d

def reference(L0_attn_x, L0_attn_Q, L0_attn_K, L0_attn_V, L0_attn_O, L0_ffn_Wr, L0_ffn_br, L0_ffn_W1, L0_ffn_b1, L0_ffn_W2, L0_ffn_b2, L0_c, L0_wmod):

    def _L0_attn_ref(x, Q, K, V, O):
        import jax, jax.numpy as jnp
        import numpy as np
        B, T, C, H = (2, 256, 128, 16)
        D_K = C // H
        d_k = Q.shape[-1]
        q = jnp.einsum('btc,chd->bhtd', x, Q)
        k = jnp.einsum('btc,chd->bhtd', x, K)
        v = jnp.einsum('btc,chd->bhtd', x, V)
        w = jnp.einsum('bhtd,bhzd->bhtz', q, k) * d_k ** 0.5
        t = w.shape[-1]
        mask = jnp.tril(jnp.ones((t, t), dtype=bool))
        w = jnp.where(mask, w, -jnp.inf)
        w = jax.nn.softmax(w, axis=-1)
        o = jnp.einsum('bhtz,bhzd->bhtd', w, v)
        b, h, tt, dk = o.shape
        o = jnp.transpose(o, (0, 2, 1, 3)).reshape(b, tt, h * dk)
        return jnp.einsum('bti,ic->btc', o, O)

    def _L0_ffn_ref(x, Wr, br, W1, b1, W2, b2):
        import jax, jax.numpy as jnp
        import numpy as np
        E = 8
        K = 2
        CAP_FACTOR = 1.0
        B, T, C = x.shape
        N = B * T
        xf = x.reshape(N, C)
        logits = xf @ Wr + br
        topv, topi = jax.lax.top_k(logits, K)
        gates = jax.nn.softmax(topv, axis=-1)
        rw = jnp.zeros((N, E), xf.dtype).at[jnp.arange(N)[:, None], topi].set(gates)
        cap = int(N * K / E * CAP_FACTOR)
        sel = jax.nn.one_hot(topi, E, dtype=jnp.int32).sum(1)
        rank = jnp.cumsum(sel, axis=0) - sel
        keep = (sel > 0) & (rank < cap)
        tok = jnp.broadcast_to(jnp.arange(N, dtype=jnp.int32)[:, None], (N, E))
        eid = jnp.broadcast_to(jnp.arange(E, dtype=jnp.int32)[None, :], (N, E))
        rank_c = jnp.where(keep, rank, cap)
        buf = jnp.full((E, cap), N, dtype=jnp.int32)
        buf = buf.at[eid, rank_c].set(tok, mode='drop')
        xpad = jnp.concatenate([xf, jnp.zeros((1, C), xf.dtype)], axis=0)
        xg = xpad[buf]
        h = jax.nn.gelu(jnp.einsum('ecd,edh->ech', xg, W1) + b1[:, None, :], approximate=False)
        out = jnp.einsum('ech,ehd->ecd', h, W2) + b2[:, None, :]
        rw_pad = jnp.concatenate([rw, jnp.zeros((1, E), rw.dtype)], axis=0)
        w = rw_pad[buf, jnp.arange(E, dtype=jnp.int32)[:, None]]
        weighted = out * w[..., None]
        final = jnp.zeros((N + 1, C), xf.dtype).at[buf.reshape(-1)].add(weighted.reshape(-1, C))
        return final[:N].reshape(B, T, C)
    x = L0_attn_x
    mod = (_silu(L0_c) @ L0_wmod).reshape(L0_c.shape[0], 6, 1, -1)
    sa, ca, ga, sb, cb, gb = (mod[:, 0], mod[:, 1], mod[:, 2], mod[:, 3], mod[:, 4], mod[:, 5])
    ga = (2 * (ga >= 0) - 1) * jnp.maximum(jnp.abs(ga), 0.25)
    gb = (2 * (gb >= 0) - 1) * jnp.maximum(jnp.abs(gb), 0.25)
    h = _layernorm(x, axis=-1) * (1 + ca) + sa
    x = x + ga * _L0_attn_ref(h, L0_attn_Q, L0_attn_K, L0_attn_V, L0_attn_O)
    h = _layernorm(x, axis=-1) * (1 + cb) + sb
    x = x + gb * _L0_ffn_ref(h, L0_ffn_Wr, L0_ffn_br, L0_ffn_W1, L0_ffn_b1, L0_ffn_W2, L0_ffn_b2)
    return x

_drawn_inputs = setup_inputs


def setup_inputs(seed=0):
    import zlib

    import numpy as np

    out = dict(_drawn_inputs(seed))
    spreads = {'L0_ffn_br': (0.0, 0.498), 'L0_ffn_b1': (0.0, 0.8), 'L0_ffn_b2': (0.0, 0.588)}
    factors = {'L0_ffn_Wr': 4.224, 'L0_ffn_W1': 7.452, 'L0_ffn_W2': 6.787}
    for name, (base, spread) in spreads.items():
        noise = np.random.default_rng([zlib.crc32(name.encode()), seed]).standard_normal(out[name].shape)
        drawn = base * np.exp(spread * noise) if base else spread * noise
        out[name] = jnp.asarray(drawn.astype(out[name].dtype))
    for name, factor in factors.items():
        out[name] = (out[name] * factor).astype(out[name].dtype)
    return out
```

```python
from contextlib import ExitStack

import concourse.bass as bass
from concourse import mybir

F32 = mybir.dt.float32
BF16 = mybir.dt.bfloat16
U32 = mybir.dt.uint32
ALU = mybir.AluOpType
ACT = mybir.ActivationFunctionType
AX = mybir.AxisListType

P = 128
B, T, C, H = 8, 512, 128, 16
D = C // H
NT = T // P
N = B * T
E = 8
FF = 512
NF = FF // P
CAP = N * 2 // E
ROW = C + 2
FAR = 1.0e6
NEG = -3.0e38
EPS = 1e-5
SCALE = float(D) ** 0.5

HALVES = 2
HH = H // HALVES
ORDER = [0, 2, 4, 6, 1, 3, 5, 7]
PARTS = 3
QROWS = PARTS * D
SROWS = 96
MROW = 96

UNITS = ([(0, p, 1) for p in range(8)] + [(1, p, 1) for p in range(8)]
         + [(2, p, 2) for p in range(0, 8, 2)] + [(3, p, 4) for p in range(0, 8, 4)])
UH = len(UNITS)
UB = HALVES * UH
GROUPS = [range(0, 4), range(4, 8), range(8, 12), range(12, 16), range(16, 20), range(20, 22)]
GB = HALVES * len(GROUPS)
AT = {7: 0, 11: 1, 15: 2, 19: 3, 21: 4, 3: 5}
SRING = 3
PRING = UH // 2


def width(kind):
    return T - P * kind


def group_of(u):
    return [n for n, g in enumerate(GROUPS) if u in g][0]


def sbank(s):
    return s % SRING if s < UB - UB % SRING else s - (UB - UB % SRING)


def sbank_before(s):
    for back in range(1, UB):
        if sbank((s - back) % UB) == sbank(s):
            return (1, s - back + UB) if s < back else (0, s - back)


def adaln_moe_kernel(nc, x, wq, wk, wv, wo, wr, br, w1, b1, w2, b2, cT, wmod, out):
    ctx = ExitStack()
    with ctx:
        def sb(name, shape, dt=F32):
            return ctx.enter_context(nc.sbuf_tensor(name, shape, dt))

        def sem(name):
            return ctx.enter_context(nc.semaphore(name))

        qd = nc.dram_tensor("q_parts_dram", [QROWS, H, T], BF16).ap()
        kd = nc.dram_tensor("k_parts_dram", [5 * D, H, T], BF16).ap()
        modd = nc.dram_tensor("mod_dram", [B, 4 * C], F32).ap()
        slots = nc.dram_tensor("slots_dram", [E * CAP, ROW], F32).ap()
        picks = nc.dram_tensor("picks_dram", [2 * N, C], F32).ap()

        xall = sb("xall", [P, B, NT, C])
        modB = sb("modB", [P, B, 4 * C])
        qrows = sb("qrows", [P, 2, H, T], BF16)
        krows = sb("krows", [P, 2, H, T], BF16)
        prob = sb("prob", [P, PRING, T])
        vpad = sb("vpad", [P, 2, NT, H, 32])
        wq_sb = sb("wq_sb", [P, C])
        wk_sb = sb("wk_sb", [P, C])
        wv_sb = sb("wv_sb", [P, C])
        wo_sb = sb("wo_sb", [P, C])
        wr_sb = sb("wr_sb", [P, E])
        br_sb = sb("br_sb", [P, E])
        b1_sb = sb("b1_sb", [P, E * NF])
        b2_sb = sb("b2_sb", [P, E, C])
        w1_sb = sb("w1_sb", [P, 2, FF])
        w2_sb = sb("w2_sb", [P, 2, NF, C])
        cT_sb = sb("cT_sb", [P, B])
        csig = sb("csig", [P, B])
        csilu = sb("csilu", [P, B])
        saT = sb("saT", [P, B])
        caT = sb("caT", [P, B])
        wmod_sb = prob[:, 0:2].rearrange("p a t -> p (a t)")[:, 0:6 * C]
        mrow = prob[0:B, 2]
        msgn = prob[0:B, 3]
        ident = sb("ident", [P, P])
        identb = sb("identb", [P, P], BF16)
        mask = sb("mask", [P, 4, P], BF16)
        upper = sb("upper", [P, P], BF16)
        onesb = sb("onesb", [P, P], BF16)
        erev = sb("erev", [P, E])
        eoff = sb("eoff", [P, E])
        tokid = sb("tokid", [P, 2, NT])
        vhalf = sb("vhalf", [P, NT])
        empty = sb("empty", [P, ROW])
        zeros = sb("zeros", [P, T])
        l1 = sb("ln1", [P, NT, C])
        l1q = sb("ln1_square", [P, NT, C])
        l1s = sb("ln1_sum", [P, 4, NT])
        l2 = sb("ln2", [P, NT, C])
        l2q = sb("ln2_square", [P, NT, C])
        l2s = sb("ln2_sum", [P, 4, NT])
        h1T = sb("h1T", [P, T])
        q32 = sb("q32", [P, T])
        k32 = sb("k32", [P, T])
        qpart = sb("qpart", [P, PARTS, T], BF16)
        kpart = sb("kpart", [P, PARTS, T], BF16)
        vtmp = sb("vtmp", [P, NT, C])
        negmax = sb("negmax", [P, 2, 4, HH])
        negrest = sb("negrest", [P, 2, 4, HH])
        mparts = sb("mparts", [P, 2, 4, PARTS, HH], BF16)
        mT = sb("mT", [PARTS * HH, 2, T], BF16)
        oS = sb("oS", [P, 2, T])
        rsum = sb("rsum", [P, 2, 16, 2])
        on = sb("on", [P, NT, C])
        oT = sb("oT", [P, T])
        proj = sb("proj", [P, NT, C])
        h2 = sb("h2", [P, NT, C])
        rows = sb("rows", [P, 2, 2, NT, ROW])
        h2T = sb("h2T", [P, T])
        lg = sb("lg", [P, NT, E])
        lg2 = sb("lg2", [P, NT, E])
        top = sb("top", [P, 2, NT])
        eq = sb("eq", [P, NT, E])
        pick = sb("pick", [P, NT, E])
        best = sb("best", [P, NT])
        hot = sb("hot", [P, 2, NT, E])
        sel = sb("sel", [P, NT, E], BF16)
        gap = sb("gap", [P, NT])
        gexp = sb("gexp", [P, NT])
        gden = sb("gden", [P, NT])
        rank = sb("rank", [P, NT, E])
        slot = sb("slot", [P, NT, E])
        carry = sb("carry", [P, E])
        prod = sb("prod", [P, 2, NT, E])
        prod2 = sb("prod2", [P, 2, NT, E])
        myrank = sb("myrank", [P, 2, NT])
        myslot = sb("myslot", [P, 2, NT])
        over = sb("over", [P, 2, NT])
        index = sb("index", [P, 2, 2, NT], U32)
        qf = qrows[:, :, :, :].rearrange("p a h t -> p (a h t)").bitcast(F32)
        kf = krows[:, :, :, :].rearrange("p a h t -> p (a h t)").bitcast(F32)
        hid = qf[:, 0:2 * NF * T].rearrange("p (a k t) -> p a k t", a=2, k=NF)
        slotT = qf[:, 4096:4096 + 2 * T].rearrange("p (a t) -> p a t", a=2)
        ysum = qf[:, 5120:5120 + T].rearrange("p (j c) -> p j c", j=NT)
        yout = qf[:, 5632:5632 + 2 * T].rearrange("p (a j c) -> p a j c", a=2, j=NT)
        two = kf.rearrange("p (b k j c) -> p b k j c", b=B, k=2, j=NT)
        slotin = qf[:, 6656:6656 + 2 * NT * ROW].rearrange("p (a j c) -> p a j c", a=2, j=NT)
        gate = sb("gate", [P, 4, NT])
        dest = sb("dest", [P, 4, NT], U32)

        ps = ctx.enter_context(nc.psum_tensor("ps", [P, 8, T], F32))
        SB_, TB, OB, M0, M1 = 0, SRING, 5, 6, 7
        m1b = ps[:, M1, :].bitcast(BF16)

        names = """x0_in x_in wqkv_in wo_in mod_w_in route_w_in b_in prefilled mod_stored modB_in
        c_exp c_one c_rec c_silu modT_mm modrow_mm mod_T mod_row mod_sgn mod_sgn1 mod_abs mod_max mod_out
        consts ident0 consts_b carry0 clear0 clear1 cleared0 cleared1 vclear vones
        s1_sum s1_cen s1_sq s1_var s1_v s1_rstd s1_norm s1_tr h1_ready
        q_mm k_mm v_mm q_copied k_copied v_copied q1 q2 q3 qr k1 k2 k3 kr v_placed
        qk_stored half0_loaded half1_loaded
        scored maxed n1 nr n2 nr2 n3 m_tr m_copied mrow0_in mrow1_in
        shifted expd masked pved o_copied o_tr o_rec o_norm oT_tr oT_copied proj_mm proj_ga x1_done
        s2_sum s2_cen s2_sq s2_var s2_v s2_rstd s2_norm h2_a h2_b rows_a rows_b h2T_tr h2T_copied logit_mm
        r_log r_top1 r_eq1 r_pick1 r_best1 r_hot1 r_log2 r_top2 r_eq2 r_pick2 r_best2 r_hot2 r_sel
        g_gap g_exp g_den g_one g_two id_set rank_mm r_rank r_carry r_slot r_prod r_prod2 r_myrank r_myslot
        r_over r_index scattered id_next
        w_in0 w_in1 slot_in0 slot_in1 slot_tr slot_T hid_mm hid_done y_mm y_add y_done gate_done dest_done picked0 picked1
        two_sum two_gb x2_done out_done""".split()
        S = {n: sem(n) for n in names}
        two_in = [sem(f"two_in{b}") for b in range(B)]

        block = ctx.enter_context(nc.Block())

        def begun(b):
            return not isinstance(b, int) or 0 <= b < B

        def earlier(b, back=1):
            return not isinstance(b, int) or b >= back

        def timeline(eng, step):
            for t in range(-2, B + 2):
                step(t, t % 2)

        @block.sync
        def _(sp):
            sp.dma_start(xall[:, 0], x[0].rearrange("(j p) c -> p j c", p=P)).then_inc(S["x0_in"], 16)
            sp.dma_start(cT_sb[:, :], cT).then_inc(S["mod_w_in"], 16)
            sp.dma_start(wmod_sb, wmod).then_inc(S["mod_w_in"], 16)
            sp.dma_start(wq_sb[:, :], wq).then_inc(S["wqkv_in"], 16)
            sp.dma_start(wk_sb[:, :], wk).then_inc(S["wqkv_in"], 16)
            sp.dma_start(wv_sb[:, :], wv).then_inc(S["wqkv_in"], 16)
            sp.dma_start(xall[:, 1:B], x[1:B].rearrange("b (j p) c -> p b j c", p=P)).then_inc(S["x_in"], 16)
            sp.dma_start(wo_sb[:, :], wo).then_inc(S["wo_in"], 16)
            sp.dma_start(wr_sb[:, :], wr).then_inc(S["route_w_in"], 16)
            sp.dma_start(br_sb[:, :], br.partition_broadcast(P)).then_inc(S["route_w_in"], 16)
            sp.dma_start(b1_sb[:, :], b1).then_inc(S["b_in"], 16)
            sp.dma_start(b2_sb[:, :, :], b2.partition_broadcast(P)).then_inc(S["b_in"], 16)
            sp.wait_ge(S["mod_out"], 3)
            sp.dma_start(modd, mrow).then_inc(S["mod_stored"], 16)
            sp.wait_ge(S["mod_stored"], 16)
            sp.dma_start(modB[:, :, :], modd.partition_broadcast(P)).then_inc(S["modB_in"], 16)
            sp.wait_ge(S["consts"], 8)
            sp.dma_start(slots.rearrange("(p n) c -> p n c", p=P),
                         empty[:, None, :].to_broadcast([P, E * CAP // P, ROW])).then_inc(S["prefilled"], 16)
            sp.dma_start(picks.rearrange("(p n m) c -> p n (m c)", p=P, m=T // C),
                         zeros[:, None, :].to_broadcast([P, 2 * N // P // 4, T])).then_inc(S["prefilled"], 16)

            def load_rows(b, par, half):
                heads = slice(half * HH, (half + 1) * HH)
                done = S["half0_loaded" if half == 0 else "half1_loaded"]
                for j in range(PARTS):
                    r = slice(j * QROWS, (j + 1) * QROWS)
                    sp.dma_start(qrows[r, par, heads], qd[:, heads]).then_inc(done, 16)
                    sp.dma_start(krows[r, par, heads], kd[j * D:j * D + QROWS, heads]).then_inc(done, 16)

            def load_maxima(b, par, half):
                heads = slice(half * HH, (half + 1) * HH)
                sp.wait_ge(S["m_copied"], 2 * b + half + 1)
                for i in range(PARTS):
                    sp.dma_start(qrows[MROW + i:MROW + i + 1, par, heads],
                                 mT[i * HH:(i + 1) * HH, half]).then_inc(S[f"mrow{half}_in"], 16)

            def step(t, u):
                prep, att = t + 2, t
                if begun(att):
                    load_maxima(att, u, 1)
                if begun(prep):
                    if earlier(prep):
                        sp.wait_ge(S["half0_loaded"], 96 * prep)
                        sp.wait_ge(S["half1_loaded"], 96 * prep)
                    sp.wait_ge(S["q3"], prep + 1)
                    sp.dma_start(qd.rearrange("(a d) h t -> (d h) a t", a=PARTS), qpart[:, :, :])\
                      .then_inc(S["qk_stored"], 16)
                    sp.wait_ge(S["k3"], prep + 1)
                    sp.dma_start(kd[0:QROWS].rearrange("(a d) h t -> (d h) a t", a=PARTS), kpart[:, :, :])\
                      .then_inc(S["qk_stored"], 16)
                    sp.dma_start(kd[QROWS:5 * D].rearrange("(a d) h t -> (d h) a t", a=2), kpart[:, 0:2, :])\
                      .then_inc(S["qk_stored"], 16)
                    sp.wait_ge(S["qk_stored"], 48 * (prep + 1))
                    if not earlier(prep, 2):
                        sp.wait_ge(S[f"cleared{u}"], 1)
                    if begun(att):
                        sp.wait_ge(S["shifted"], UB * att + UH)
                    load_rows(prep, u, 0)
                if begun(t + 1):
                    load_maxima(t + 1, 1 - u, 0)
                if begun(prep):
                    if begun(att):
                        sp.wait_ge(S["shifted"], UB * att + UB)
                    load_rows(prep, u, 1)

            timeline(sp, step)

            def load_slots(n, q, e):
                if earlier(n, 2):
                    sp.wait_ge(S["slot_tr"], n - 1)
                    sp.wait_ge(S["dest_done"], n - 1)
                sp.dma_start(slotin[:, q % 2], slots[bass.ds(n * T, T), :].rearrange("(j p) c -> p j c", p=P))\
                  .then_inc(S[f"slot_in{q % 2}"], 16)

            def load_expert(e, par):
                if earlier(e, 2):
                    sp.wait_ge(S["y_mm"], 2 * e - 2)
                sp.dma_start(w1_sb[:, par], w1[e]).then_inc(S[f"w_in{par}"], 16)
                sp.dma_start(w2_sb[:, par], w2[e].rearrange("(k p) c -> p k c", p=P)).then_inc(S[f"w_in{par}"], 16)

            load_expert(0, 0)
            load_expert(1, 1)
            sp.wait_ge(S["scattered"], 16 * 2 * NT * B)
            for n in range(4):
                load_slots(n, n, n // 2)
            with sp.Fori(1, E // 2) as i:
                for q in range(4):
                    if q % 2 == 0:
                        load_expert(2 * i + q // 2, q // 2)
                    load_slots(4 * i + q, q, 2 * i + q // 2)

            for par in range(2):
                sp.wait_ge(S[f"picked{par}"], 16 * NT * E)
            pv = picks.rearrange("(k b j p) c -> b k p j c", k=2, b=B, p=P)
            for b in range(B):
                for k in range(2):
                    sp.dma_start(two[:, b, k], pv[b, k]).then_inc(two_in[b], 16)
            with sp.Fori(0, B) as b:
                sp.wait_ge(S["x2_done"], b + 1)
                sp.dma_start(out[b].rearrange("(j p) c -> p j c", p=P), xall[:, b]).then_inc(S["out_done"], 16)
            sp.wait_ge(S["out_done"], 16 * B)

        @block.tensor
        def _(pe):
            mm = nc.tensor.matmul
            pe.wait_ge(S["mod_w_in"], 32)
            pe.wait_ge(S["c_silu"], 1)
            for j in range(2):
                last = mm(ps[:, M0, j * B:(j + 1) * B], wmod_sb[:, j * C:(j + 1) * C], csilu[:, :],
                          start=True, stop=True)
            last.then_inc(S["modT_mm"], 1)
            mm(ps[0:B, M1, :], csilu[:, :], wmod_sb[:, 2 * C:6 * C], start=True, stop=True)\
                .then_inc(S["modrow_mm"], 1)
            pe.wait_ge(S["consts"], 8)
            pe.wait_ge(S["wqkv_in"], 48)
            pe.wait_ge(S["mod_T"], 2)
            pe.wait_ge(S["mod_row"], 1)

            def prepare(b, u, s):
                if s == 11:
                    pe.wait_ge(S["s1_norm"], b + 1)
                    if begun(b - 2):
                        pe.wait_ge(S["m_copied"], 2 * b - 2)
                    elif earlier(b):
                        pe.wait_ge(S["v_copied"], b)
                    for j in range(NT):
                        last = nc.tensor.transpose(ps[:, M1, j * P:(j + 1) * P], l1[:, j, :], ident[:, :])
                    last.then_inc(S["s1_tr"], 1)
                if s == 14:
                    pe.wait_ge(S["h1_ready"], b + 1)
                    mm(ps[:, M1, :], wq_sb[:, :], h1T[:, :], start=True, stop=True).then_inc(S["q_mm"], 1)
                if s == 17:
                    pe.wait_ge(S["q_copied"], b + 1)
                    mm(ps[:, M1, :], wk_sb[:, :], h1T[:, :], start=True, stop=True).then_inc(S["k_mm"], 1)
                if s == 20:
                    pe.wait_ge(S["k_copied"], b + 1)
                    for j in range(NT):
                        last = mm(ps[:, M1, j * P:(j + 1) * P], h1T[:, j * P:(j + 1) * P], wv_sb[:, :],
                                  start=True, stop=True)
                    last.then_inc(S["v_mm"], 1)

            def maxima_T(b, half):
                pe.wait_ge(S["n3"], 2 * b + half + 1)
                for j in range(NT):
                    last = nc.tensor.transpose(m1b[0:PARTS * HH, j * P:(j + 1) * P],
                                               mparts[:, half, j].rearrange("p a h -> p (a h)"), identb[:, :])
                last.then_inc(S["m_tr"], 1)

            def score(b, u, s):
                half, (kind, pos, nh) = s // UH, UNITS[s % UH]
                qb = NT - 1 - kind
                w = width(kind)
                if s % UH == 0:
                    pe.wait_ge(S[f"half{half}_loaded"], 96 * (b + 1))
                back, before = sbank_before(s)
                if not back or earlier(b):
                    pe.wait_ge(S["maxed"], UB * (b - back) + before + 1)
                bank = ps[:, SB_ + sbank(s), :]
                for i in range(nh):
                    h = half * HH + pos + i
                    mm(bank[:, i * w:(i + 1) * w], qrows[0:SROWS, u, h, qb * P:(qb + 1) * P],
                       krows[0:SROWS, u, h, 0:w], start=(i == 0), stop=False, skip_group_check=True)
                diag = bank[:, 0:nh * w].rearrange("p (n w) -> p n w", n=nh)[:, :, qb * P:w]
                mm(diag, identb[:, :], mask[:, 0:nh, :], start=False, stop=True,
                   skip_group_check=True).then_inc(S["scored"], 1)

            def shifted(b, u, s):
                half, (kind, pos, nh) = s // UH, UNITS[s % UH]
                w = width(kind)
                if s % UH == 0:
                    pe.wait_ge(S[f"mrow{half}_in"], 48 * (b + 1))
                if s >= 2 or earlier(b):
                    pe.wait_ge(S["expd"], UB * b + s - 1)
                bank = ps[:, TB + s % 2, :]
                for i in range(nh):
                    h = half * HH + pos + i
                    last = mm(bank[:, i * w:(i + 1) * w], krows[:, u, h, kind * P:(kind + 1) * P],
                              qrows[:, u, h, kind * P:T], start=True, stop=True)
                last.then_inc(S["shifted"], 1)

            def values(b, u, half, g):
                if g == 0:
                    if half == 0:
                        pe.wait_ge(S["v_placed"], b + 1)
                    if half or earlier(b):
                        pe.wait_ge(S["o_copied"], 2 * b + half)
                pe.wait_ge(S["masked"], UB * b + UH * half + GROUPS[g][-1] + 1)
                for v in GROUPS[g]:
                    kind, pos, nh = UNITS[v]
                    w = width(kind)
                    for i in range(nh):
                        grp, slt = (pos + i) % 4, (pos + i) // 4
                        head = half * HH + ORDER[pos + i]
                        last = mm(ps[32 * grp:32 * grp + 32, OB, kind * P:T], vpad[:, u, kind, head, :],
                                  prob[:, (half * UH + v) % PRING, i * w:(i + 1) * w],
                                  start=(kind == 0 and slt == 0), stop=(kind == 3 and slt == 1),
                                  skip_group_check=True)
                last.then_inc(S["pved"], 1)

            def sums_T(b, half):
                pe.wait_ge(S["o_copied"], 2 * b + half + 1)
                for j in range(NT):
                    last = nc.tensor.transpose(ps[:, M0, j * P:(j + 1) * P], oS[:, half, j * P:(j + 1) * P],
                                               ident[:, :])
                last.then_inc(S["o_tr"], 1)

            def output(b, u, s):
                if s == 6:
                    if earlier(b):
                        pe.wait_ge(S["r_log"], b)
                    pe.wait_ge(S["o_norm"], 4 * b + 2)
                    sums_T(b, 1)
                if s == 12:
                    pe.wait_ge(S["o_norm"], 4 * b + 4)
                    for j in range(NT):
                        last = nc.tensor.transpose(ps[:, M0, j * P:(j + 1) * P], on[:, j, :], ident[:, :])
                    last.then_inc(S["oT_tr"], 1)
                if s == 19:
                    if not earlier(b):
                        pe.wait_ge(S["wo_in"], 16)
                    pe.wait_ge(S["oT_copied"], b + 1)
                    if earlier(b):
                        pe.wait_ge(S["r_carry"], b)
                    for j in range(NT):
                        last = mm(ps[:, M0, j * P:(j + 1) * P], oT[:, j * P:(j + 1) * P], wo_sb[:, :],
                                  start=True, stop=True)
                    last.then_inc(S["proj_mm"], 1)
                if s == 37:
                    pe.wait_ge(S["h2_b"], b + 1)
                    if begun(b + 1):
                        pe.wait_ge(S["o_norm"], 4 * b + 6)
                    for j in range(NT):
                        last = nc.tensor.transpose(ps[:, M0, j * P:(j + 1) * P], rows[:, u, 0, j, 0:C],
                                                   ident[:, :])
                    last.then_inc(S["h2T_tr"], 1)
                if s == 41:
                    if not earlier(b):
                        pe.wait_ge(S["route_w_in"], 32)
                    pe.wait_ge(S["h2T_copied"], b + 1)
                    for j in range(NT):
                        last = mm(ps[:, M0, j * E:(j + 1) * E], h2T[:, j * P:(j + 1) * P], wr_sb[:, :],
                                  start=True, stop=True)
                    last.then_inc(S["logit_mm"], 1)

            def route(b, u, s):
                if s == 15:
                    pe.wait_ge(S["r_sel"], b + 1)
                    pe.wait_ge(S["r_log"], b + 1)
                    if begun(b + 1):
                        pe.wait_ge(S["oT_copied"], b + 2)
                    for j in range(NT + 1):
                        reg = ps[:, M0, j * E:(j + 1) * E]
                        for k in range(j):
                            last = mm(reg, onesb[:, :], sel[:, k, :], start=(k == 0), stop=(j == NT and k == j - 1))
                        if j < NT:
                            last = mm(reg, upper[:, :], sel[:, j, :], start=(j == 0), stop=True)
                    last.then_inc(S["rank_mm"], 1)

            def step(t, u):
                for s in range(UB):
                    if begun(t + 2):
                        prepare(t + 2, u, s)
                    if begun(t - 1):
                        output(t - 1, 1 - u, s)
                    if begun(t - 2):
                        route(t - 2, u, s)
                    if s == 5 and begun(t):
                        pe.wait_ge(S["m_copied"], 2 * t + 1)
                        maxima_T(t, 1)
                    if s == 28 and begun(t):
                        if begun(t - 1):
                            pe.wait_ge(S["proj_ga"], t)
                        sums_T(t, 0)
                    if s == 30 and begun(t + 1):
                        if begun(t + 2):
                            pe.wait_ge(S["v_copied"], t + 3)
                        else:
                            pe.wait_ge(S["m_copied"], 2 * t + 2)
                        maxima_T(t + 1, 0)
                    if begun(t + 1):
                        score(t + 1, 1 - u, s)
                    if begun(t):
                        shifted(t, u, s)
                    half, v = divmod(s, UH)
                    if v in AT:
                        g = AT[v]
                        if g < 5 and begun(t):
                            values(t, u, half, g)
                        if g == 5 and half == 1 and begun(t):
                            values(t, u, 0, g)
                        if g == 5 and half == 0 and begun(t - 1):
                            values(t - 1, 1 - u, 1, g)

            timeline(pe, step)

            def up(n, q, pair):
                if q % 2 == 0:
                    pe.wait_ge(S[f"w_in{q // 2}"], 32 * (pair + 1))
                pe.wait_ge(S["slot_T"], n + 1)
                for k in range(NF):
                    if earlier(n):
                        pe.wait_ge(S["hid_done"], NF * (n - 1) + k + 1)
                    mm(ps[:, k, :], w1_sb[:, q // 2, k * P:(k + 1) * P], slotT[:, q % 2, :],
                       start=True, stop=True).then_inc(S["hid_mm"], 1)

            def slots_T(n, q, e):
                pe.wait_ge(S[f"slot_in{q % 2}"], 16 * (e + 1))
                if earlier(n):
                    pe.wait_ge(S["slot_T"], n)
                for j in range(NT):
                    last = nc.tensor.transpose(ps[:, 6, j * P:(j + 1) * P], slotin[:, q % 2, j, 0:C], ident[:, :])
                last.then_inc(S["slot_tr"], 1)

            def down(n, q, e):
                pe.wait_ge(S["hid_done"], NF * (n + 1))
                if earlier(n, 2):
                    pe.wait_ge(S["y_add"], n - 1)
                for j in range(NT):
                    for k in range(NF):
                        last = mm(ps[:, 4 + q % 2, j * P:(j + 1) * P], hid[:, q % 2, k, j * P:(j + 1) * P],
                                  w2_sb[:, q // 2, k, :], start=(k == 0), stop=(k == NF - 1))
                last.then_inc(S["y_mm"], 1)

            pe.wait_ge(S["r_carry"], B)
            pe.wait_ge(S["maxed"], UB * B)
            pe.wait_ge(S["expd"], UB * B)
            pe.wait_ge(S["o_copied"], 2 * B)
            slots_T(0, 0, 0)
            slots_T(1, 1, 0)
            up(0, 0, 0)
            for n in range(4):
                up(n + 1, (n + 1) % 4, (n + 1) // 4)
                slots_T(n + 2, (n + 2) % 4, (n + 2) // 2)
                down(n, n, n // 2)
            with pe.Fori(1, E // 2 - 1) as i:
                for q in range(4):
                    up(4 * i + q + 1, (q + 1) % 4, i + (q + 1) // 4)
                    slots_T(4 * i + q + 2, (q + 2) % 4, 2 * i + (q + 2) // 2)
                    down(4 * i + q, q, 2 * i + q // 2)
            for n in range(2 * E - 4, 2 * E):
                if n + 1 < 2 * E:
                    up(n + 1, (n + 1) % 4, (n + 1) // 4)
                if n + 2 < 2 * E:
                    slots_T(n + 2, (n + 2) % 4, (n + 2) // 2)
                down(n, n % 4, n // 2)

        @block.scalar
        def _(act):
            fn = nc.scalar.activation
            act.wait_ge(S["mod_w_in"], 32)
            fn(csig[:, :], cT_sb[:, :], ACT.Exp, scale=-1.0).then_inc(S["c_exp"], 1)
            act.wait_ge(S["modrow_mm"], 1)
            fn(mrow, ps[0:B, M1, :], ACT.Copy).then_inc(S["mod_row"], 1)
            act.wait_ge(S["mod_T"], 2)

            def prepare(b, u, s):
                if s == 3:
                    act.wait_ge(S["s1_cen"], b + 1)
                    if earlier(b):
                        act.wait_ge(S["s1_var"], b)
                    fn(l1q[:, :, :], l1[:, :, :], ACT.Square).then_inc(S["s1_sq"], 1)
                if s == 12:
                    act.wait_ge(S["s1_tr"], b + 1)
                    fn(h1T[:, :], ps[:, M1, :], ACT.Identity, bias=saT[:, bass.ds(b, 1)],
                       scale=caT[:, bass.ds(b, 1)]).then_inc(S["h1_ready"], 1)
                if s == 15:
                    act.wait_ge(S["q_mm"], b + 1)
                    if earlier(b):
                        act.wait_ge(S["q3"], b)
                    fn(q32[:, :], ps[:, M1, :], ACT.Copy).then_inc(S["q_copied"], 1)
                if s == 18:
                    act.wait_ge(S["k_mm"], b + 1)
                    if earlier(b):
                        act.wait_ge(S["k3"], b)
                    fn(k32[:, :], ps[:, M1, :], ACT.Copy).then_inc(S["k_copied"], 1)
                if s == 21:
                    act.wait_ge(S["v_mm"], b + 1)
                    if earlier(b):
                        act.wait_ge(S["v_placed"], b)
                    fn(vtmp[:, :, :], ps[:, M1, :].rearrange("p (j c) -> p j c", j=NT), ACT.Copy)\
                        .then_inc(S["v_copied"], 1)

            def copy_maxima(b, half):
                act.wait_ge(S["m_tr"], 2 * b + half + 1)
                if earlier(b):
                    act.wait_ge(S[f"mrow{half}_in"], 48 * b)
                fn(mT[:, half, :], m1b[0:PARTS * HH, 0:T], ACT.Copy).then_inc(S["m_copied"], 1)

            def exps(b, u, s):
                half, (kind, pos, nh) = s // UH, UNITS[s % UH]
                w = nh * width(kind)
                if s == 0 and not earlier(b):
                    act.wait_ge(S["mod_stored"], 16)
                act.wait_ge(S["shifted"], UB * b + s + 1)
                v = s - PRING
                if v >= 0:
                    act.wait_ge(S["pved"], GB * b + len(GROUPS) * (v // UH) + group_of(v % UH) + 1)
                elif earlier(b):
                    act.wait_ge(S["pved"], GB * (b - 1) + len(GROUPS) + group_of((v + UB) % UH) + 1)
                fn(prob[:, s % PRING, 0:w], ps[:, TB + s % 2, 0:w], ACT.Exp, scale=SCALE)\
                    .then_inc(S["expd"], 1)

            def copy_sums(b, half):
                act.wait_ge(S["pved"], GB * b + len(GROUPS) * (half + 1))
                if earlier(b):
                    act.wait_ge(S["o_tr"], 2 * b + half - 1)
                fn(oS[:, half, :], ps[:, OB, :], ACT.Copy).then_inc(S["o_copied"], 1)

            def output(b, u, s):
                if s == 4:
                    copy_sums(b, 1)
                if s == 13:
                    act.wait_ge(S["oT_tr"], b + 1)
                    if earlier(b):
                        act.wait_ge(S["proj_mm"], b)
                    fn(oT[:, :], ps[:, M0, :], ACT.Copy).then_inc(S["oT_copied"], 1)
                if s == 27:
                    act.wait_ge(S["s2_cen"], b + 1)
                    if earlier(b):
                        act.wait_ge(S["s2_var"], b)
                    fn(l2q[:, :, :], l2[:, :, :], ACT.Square).then_inc(S["s2_sq"], 1)
                if s == 36:
                    act.wait_ge(S["h2_b"], b + 1)
                    if earlier(b, 2):
                        act.wait_ge(S["scattered"], 16 * 2 * NT * (b - 1))
                    fn(rows[:, u, 1, :, 0:C], rows[:, u, 0, :, 0:C], ACT.Copy).then_inc(S["rows_b"], 1)
                if s == 38:
                    act.wait_ge(S["h2T_tr"], b + 1)
                    if earlier(b):
                        act.wait_ge(S["logit_mm"], b)
                    fn(h2T[:, :], ps[:, M0, :], ACT.Copy).then_inc(S["h2T_copied"], 1)

            def route(b, u, s):
                if s == 10:
                    act.wait_ge(S["g_gap"], b + 1)
                    if earlier(b):
                        act.wait_ge(S["g_two"], b)
                    fn(gexp[:, :], gap[:, :], ACT.Exp).then_inc(S["g_exp"], 1)

            def step(t, u):
                for s in range(UB):
                    if begun(t):
                        exps(t, u, s)
                    if begun(t + 2):
                        prepare(t + 2, u, s)
                    if begun(t - 1):
                        output(t - 1, 1 - u, s)
                    if begun(t - 2):
                        route(t - 2, u, s)
                    if s == 6 and begun(t):
                        copy_maxima(t, 1)
                    if s == 26 and begun(t):
                        copy_sums(t, 0)
                    if s == 31 and begun(t + 1):
                        copy_maxima(t + 1, 0)

            timeline(act, step)

            def gelu(n, q, e):
                if not earlier(n):
                    act.wait_ge(S["b_in"], 32)
                if earlier(n, 2):
                    act.wait_ge(S["y_mm"], n - 1)
                for k in range(NF):
                    act.wait_ge(S["hid_mm"], NF * n + k + 1)
                    fn(hid[:, q % 2, k, :], ps[:, k, :], ACT.Gelu,
                       bias=b1_sb[:, bass.ds(NF * e + k, 1)]).then_inc(S["hid_done"], 1)

            for n in range(2 * E):
                gelu(n, n % 4, n // 2)

        @block.vector
        def _(dve):
            tt, ts, red = nc.vector.tensor_tensor, nc.vector.tensor_scalar, nc.vector.tensor_reduce
            stt, cp = nc.vector.scalar_tensor_tensor, nc.vector.tensor_copy

            dve.wait_ge(S["c_exp"], 1)
            ts(csig[:, :], csig[:, :], 1.0, None, ALU.add).then_inc(S["c_one"], 1)
            dve.wait_ge(S["c_one"], 1)
            nc.vector.reciprocal(csig[:, :], csig[:, :]).then_inc(S["c_rec"], 1)
            dve.wait_ge(S["c_rec"], 1)
            dve.wait_ge(S["mod_w_in"], 32)
            tt(csilu[:, :], csig[:, :], cT_sb[:, :], ALU.mult).then_inc(S["c_silu"], 1)
            dve.wait_ge(S["modT_mm"], 1)
            cp(saT[:, :], ps[:, M0, 0:B]).then_inc(S["mod_T"], 1)
            ts(caT[:, :], ps[:, M0, B:2 * B], 1.0, None, ALU.add).then_inc(S["mod_T"], 1)
            dve.wait_ge(S["mod_row"], 1)
            ts(msgn, mrow, 0.0, 2.0, ALU.is_ge, ALU.mult).then_inc(S["mod_sgn"], 1)
            dve.wait_ge(S["mod_sgn"], 1)
            ts(msgn, msgn, 1.0, None, ALU.subtract).then_inc(S["mod_sgn1"], 1)
            dve.wait_ge(S["mod_sgn1"], 1)
            for n, (a, z) in enumerate(((0, C), (3 * C, 4 * C))):
                tt(mrow[:, a:z], mrow[:, a:z], msgn[:, a:z], ALU.mult).then_inc(S["mod_abs"], 1)
                dve.wait_ge(S["mod_abs"], n + 1)
                ts(mrow[:, a:z], mrow[:, a:z], 0.25, None, ALU.max).then_inc(S["mod_max"], 1)
                dve.wait_ge(S["mod_max"], n + 1)
                tt(mrow[:, a:z], mrow[:, a:z], msgn[:, a:z], ALU.mult).then_inc(S["mod_out"], 1)
            ts(mrow[:, 2 * C:3 * C], mrow[:, 2 * C:3 * C], 1.0, None, ALU.add).then_inc(S["mod_out"], 1)
            nc.vector.memset(carry[:, :], 0.0).then_inc(S["carry0"], 1)
            dve.wait_ge(S["carry0"], 1)
            dve.wait_ge(S["consts_b"], 2)

            def prepare(b, u, s):
                if s == 0:
                    if isinstance(b, int) and b < 2:
                        dve.wait_ge(S["x_in" if b else "x0_in"], 16)
                    if earlier(b):
                        dve.wait_ge(S["s1_cen"], b)
                    red(l1s[:, 0, :], xall[:, b], AX.X, ALU.add).then_inc(S["s1_sum"], 1)
                if s == 2:
                    dve.wait_ge(S["s1_sum"], b + 1)
                    if earlier(b):
                        dve.wait_ge(S["s1_tr"], b)
                    stt(l1[:, :, :], l1s[:, 0, :].unsqueeze(2).to_broadcast([P, NT, C]), -1.0 / C, xall[:, b],
                        ALU.mult, ALU.add).then_inc(S["s1_cen"], 1)
                if s == 5:
                    dve.wait_ge(S["s1_sq"], b + 1)
                    if earlier(b):
                        dve.wait_ge(S["s1_v"], b)
                    red(l1s[:, 1, :], l1q[:, :, :], AX.X, ALU.add).then_inc(S["s1_var"], 1)
                if s == 9:
                    dve.wait_ge(S["s1_rstd"], b + 1)
                    tt(l1[:, :, :], l1[:, :, :], l1s[:, 3, :].unsqueeze(2).to_broadcast([P, NT, C]), ALU.mult)\
                        .then_inc(S["s1_norm"], 1)
                for (z, z32, part, s1) in (("q", q32, qpart, 16), ("k", k32, kpart, 20)):
                    if s == s1:
                        dve.wait_ge(S[z + "_copied"], b + 1)
                        if earlier(b):
                            dve.wait_ge(S["qk_stored"], 48 * b)
                        cp(part[:, 0, :], z32[:, :]).then_inc(S[z + "1"], 1)
                    if s == s1 + 3:
                        dve.wait_ge(S[z + "r"], b + 1)
                        cp(part[:, 1, :], z32[:, :]).then_inc(S[z + "2"], 1)

            def maximum(b, s):
                half, (kind, pos, nh) = s // UH, UNITS[s % UH]
                w = width(kind)
                dve.wait_ge(S["scored"], UB * b + s + 1)
                if s % UH == 0 and earlier(b):
                    dve.wait_ge(S["nr"], 2 * b + half - 1)
                red(negmax[:, half, NT - 1 - kind, pos:pos + nh],
                    ps[:, SB_ + sbank(s), 0:nh * w].rearrange("p (n w) -> p n w", n=nh),
                    AX.X, ALU.max, negate=True).then_inc(S["maxed"], 1)

            def split_maxima(b, half, n):
                z = 2 * b + half
                def part(i):
                    return mparts[:, half, :, i, :]
                if n == 0:
                    dve.wait_ge(S["maxed"], UB * b + UH * (half + 1))
                    if earlier(b):
                        dve.wait_ge(S["m_tr"], z - 1)
                    cp(part(0), negmax[:, half]).then_inc(S["n1"], 1)
                if n == 1:
                    dve.wait_ge(S["n1"], z + 1)
                    tt(negrest[:, half], negmax[:, half], part(0), ALU.subtract).then_inc(S["nr"], 1)
                if n == 2:
                    dve.wait_ge(S["nr"], z + 1)
                    cp(part(1), negrest[:, half]).then_inc(S["n2"], 1)
                if n == 3:
                    dve.wait_ge(S["n2"], z + 1)
                    tt(part(2), negrest[:, half], part(1), ALU.subtract).then_inc(S["n3"], 1)

            def normalise(b, half, n):
                z = 2 * b + half
                sums = ps[:, M0, :].rearrange("p (x c) -> p x c", c=32)
                if n == 0:
                    dve.wait_ge(S["o_tr"], z + 1)
                    if earlier(b):
                        dve.wait_ge(S["o_norm"], 2 * z - 2)
                    nc.vector.reciprocal(rsum[:, half], sums[:, :, D:2 * D + 2:D + 1]).then_inc(S["o_rec"], 1)
                else:
                    dve.wait_ge(S["o_rec"], z + 1)
                    if earlier(b):
                        dve.wait_ge(S["oT_tr"], b)
                    i = n - 1
                    dst = on[:, :, half * 64:half * 64 + 64].rearrange("p j (g c) -> p j g c", g=4)
                    src = sums.rearrange("p (j g) c -> p j g c", g=4)
                    rs = rsum[:, half].rearrange("p (j g) i -> p j g i", g=4)
                    tt(dst[:, :, :, D * i:D * i + D], src[:, :, :, (D + 1) * i:(D + 1) * i + D],
                       rs[:, :, :, i:i + 1].to_broadcast([P, NT, 4, D]), ALU.mult).then_inc(S["o_norm"], 1)

            def output(b, u, s):
                if s in (8, 9, 10):
                    normalise(b, 1, s - 8)
                if s == 21:
                    dve.wait_ge(S["proj_mm"], b + 1)
                    if not earlier(b):
                        dve.wait_ge(S["modB_in"], 16)
                    if earlier(b):
                        dve.wait_ge(S["x1_done"], b)
                    tt(proj[:, :, :], ps[:, M0, :].rearrange("p (j c) -> p j c", j=NT),
                       modB[:, bass.ds(b, 1), 0:C].to_broadcast([P, NT, C]), ALU.mult).then_inc(S["proj_ga"], 1)
                if s == 24:
                    dve.wait_ge(S["x1_done"], b + 1)
                    if earlier(b):
                        dve.wait_ge(S["s2_cen"], b)
                    red(l2s[:, 0, :], xall[:, b], AX.X, ALU.add).then_inc(S["s2_sum"], 1)
                if s == 26:
                    dve.wait_ge(S["s2_sum"], b + 1)
                    if earlier(b):
                        dve.wait_ge(S["h2_a"], b)
                    stt(l2[:, :, :], l2s[:, 0, :].unsqueeze(2).to_broadcast([P, NT, C]), -1.0 / C, xall[:, b],
                        ALU.mult, ALU.add).then_inc(S["s2_cen"], 1)
                if s == 29:
                    dve.wait_ge(S["s2_sq"], b + 1)
                    if earlier(b):
                        dve.wait_ge(S["s2_v"], b)
                    red(l2s[:, 1, :], l2q[:, :, :], AX.X, ALU.add).then_inc(S["s2_var"], 1)
                if s == 32:
                    dve.wait_ge(S["s2_rstd"], b + 1)
                    tt(l2[:, :, :], l2[:, :, :], l2s[:, 3, :].unsqueeze(2).to_broadcast([P, NT, C]), ALU.mult)\
                        .then_inc(S["s2_norm"], 1)

            def over_experts(v):
                return v.unsqueeze(2).to_broadcast([P, NT, E])

            def over_tiles(v):
                return v.unsqueeze(1).to_broadcast([P, NT, E])

            def route(b, u, s):
                if s == 0:
                    dve.wait_ge(S["logit_mm"], b + 1)
                    if earlier(b):
                        dve.wait_ge(S["r_log2"], b)
                    tt(lg[:, :, :], ps[:, M0, 0:NT * E].rearrange("p (j e) -> p j e", j=NT),
                       over_tiles(br_sb[:, :]), ALU.add).then_inc(S["r_log"], 1)
                for k, (s0, src) in enumerate(((1, lg), (7, lg2))):
                    z = str(k + 1)
                    prev = "r_log" if k == 0 else "r_log2"
                    if s == s0:
                        dve.wait_ge(S[prev], b + 1)
                        if earlier(b):
                            dve.wait_ge(S["g_gap"], b)
                        red(top[:, k, :], src[:, :, :], AX.X, ALU.max).then_inc(S["r_top" + z], 1)
                    if s == s0 + 1:
                        dve.wait_ge(S["r_top" + z], b + 1)
                        tt(eq[:, :, :], src[:, :, :], over_experts(top[:, k, :]), ALU.is_equal)\
                            .then_inc(S["r_eq" + z], 1)
                    if s == s0 + 2:
                        dve.wait_ge(S["r_eq" + z], b + 1)
                        tt(pick[:, :, :], eq[:, :, :], over_tiles(erev[:, :]), ALU.mult).then_inc(S["r_pick" + z], 1)
                    if s == s0 + 3:
                        dve.wait_ge(S["r_pick" + z], b + 1)
                        red(best[:, :], pick[:, :, :], AX.X, ALU.max).then_inc(S["r_best" + z], 1)
                    if s == s0 + 4:
                        dve.wait_ge(S["r_best" + z], b + 1)
                        if earlier(b):
                            dve.wait_ge(S["r_prod2"], b)
                        tt(hot[:, k], over_tiles(erev[:, :]), over_experts(best[:, :]), ALU.is_equal)\
                            .then_inc(S["r_hot" + z], 1)
                if s == 6:
                    dve.wait_ge(S["r_hot1"], b + 1)
                    stt(lg2[:, :, :], hot[:, 0], NEG, lg[:, :, :], ALU.mult, ALU.add).then_inc(S["r_log2"], 1)
                if s == 8:
                    dve.wait_ge(S["r_top2"], b + 1)
                    if earlier(b):
                        dve.wait_ge(S["g_exp"], b)
                    tt(gap[:, :], top[:, 1, :], top[:, 0, :], ALU.subtract).then_inc(S["g_gap"], 1)
                if s == 12:
                    dve.wait_ge(S["r_hot2"], b + 1)
                    if earlier(b):
                        dve.wait_ge(S["rank_mm"], b)
                    tt(sel[:, :, :], hot[:, 0], hot[:, 1], ALU.add).then_inc(S["r_sel"], 1)
                    dve.wait_ge(S["g_exp"], b + 1)
                    ts(gden[:, :], gexp[:, :], 1.0, None, ALU.add).then_inc(S["g_den"], 1)
                if s == 14:
                    dve.wait_ge(S["g_den"], b + 1)
                    if earlier(b):
                        dve.wait_ge(S["scattered"], 16 * 2 * NT * b)
                    nc.vector.reciprocal(rows[:, u, 0, :, C], gden[:, :]).then_inc(S["g_one"], 1)
                if s == 15:
                    dve.wait_ge(S["g_one"], b + 1)
                    tt(rows[:, u, 1, :, C], gexp[:, :], rows[:, u, 0, :, C], ALU.mult).then_inc(S["g_two"], 1)
                if s == 17:
                    dve.wait_ge(S["rank_mm"], b + 1)
                    if earlier(b):
                        dve.wait_ge(S["r_prod"], b)
                        dve.wait_ge(S["r_carry"], b)
                    tt(rank[:, :, :], ps[:, M0, 0:NT * E].rearrange("p (j e) -> p j e", j=NT),
                       over_tiles(carry[:, :]), ALU.add).then_inc(S["r_rank"], 1)
                    dve.wait_ge(S["r_rank"], b + 1)
                    tt(carry[:, :], ps[:, M0, NT * E:(NT + 1) * E], carry[:, :], ALU.add)\
                        .then_inc(S["r_carry"], 1)
                if s == 18:
                    dve.wait_ge(S["r_rank"], b + 1)
                    if earlier(b):
                        dve.wait_ge(S["r_prod2"], b)
                    tt(slot[:, :, :], rank[:, :, :], over_tiles(eoff[:, :]), ALU.add).then_inc(S["r_slot"], 1)
                if s == 19:
                    if earlier(b):
                        dve.wait_ge(S["r_myrank"], b)
                        dve.wait_ge(S["r_myslot"], b)
                    dve.wait_ge(S["r_hot2"], b + 1)
                    for k in range(2):
                        last = tt(prod[:, k], hot[:, k], rank[:, :, :], ALU.mult)
                    last.then_inc(S["r_prod"], 1)
                if s == 20:
                    dve.wait_ge(S["r_slot"], b + 1)
                    for k in range(2):
                        last = tt(prod2[:, k], hot[:, k], slot[:, :, :], ALU.mult)
                    last.then_inc(S["r_prod2"], 1)
                if s == 21:
                    dve.wait_ge(S["r_prod"], b + 1)
                    if earlier(b):
                        dve.wait_ge(S["r_over"], b)
                    red(myrank[:, :, :], prod[:, :, :, :], AX.X, ALU.add).then_inc(S["r_myrank"], 1)
                if s == 22:
                    dve.wait_ge(S["r_prod2"], b + 1)
                    if earlier(b):
                        dve.wait_ge(S["r_index"], b)
                    red(myslot[:, :, :], prod2[:, :, :, :], AX.X, ALU.add).then_inc(S["r_myslot"], 1)
                if s == 23:
                    dve.wait_ge(S["r_myrank"], b + 1)
                    ts(over[:, :, :], myrank[:, :, :], float(CAP), FAR, ALU.is_ge, ALU.mult).then_inc(S["r_over"], 1)
                if s == 24:
                    dve.wait_ge(S["r_over"], b + 1)
                    dve.wait_ge(S["r_myslot"], b + 1)
                    if earlier(b):
                        dve.wait_ge(S["scattered"], 16 * 2 * NT * b)
                    tt(index[:, u], myslot[:, :, :], over[:, :, :], ALU.add).then_inc(S["r_index"], 1)

            def step(t, u):
                for s in range(UB):
                    if isinstance(t, int) and t == -2 and s in (10, 26):
                        z = s // 26
                        nc.vector.memset(qrows[64:P, z].bitcast(U32), 0).then_inc(S[f"clear{z}"], 1)
                    if isinstance(t, int) and t == -2 and s in (30, 43):
                        z = s // 43
                        dve.wait_ge(S[f"clear{z}"], 2)
                        nc.vector.memset(krows[MROW:MROW + PARTS, z, :, :], 1.0).then_inc(S[f"cleared{z}"], 1)
                    if begun(t + 1):
                        maximum(t + 1, s)
                    if s < 4 and begun(t):
                        split_maxima(t, 1, s)
                    if 23 <= s < 27 and begun(t + 1):
                        split_maxima(t + 1, 0, s - 23)
                    if begun(t - 2):
                        route(t - 2, u, s)
                    if begun(t + 2):
                        prepare(t + 2, u, s)
                    if begun(t - 1):
                        output(t - 1, 1 - u, s)
                    if s in (30, 31, 33) and begun(t):
                        normalise(t, 0, (30, 31, 33).index(s))

            timeline(dve, step)

            def slots_copy(n, q, e):
                dve.wait_ge(S["slot_tr"], n + 1)
                if earlier(n, 2):
                    dve.wait_ge(S["hid_mm"], NF * (n - 1))
                cp(slotT[:, q % 2, :], ps[:, 6, :]).then_inc(S["slot_T"], 1)
                if earlier(n, 4):
                    dve.wait_ge(S[f"picked{q % 2}"], 16 * NT * (e - 1))
                    dve.wait_ge(S["y_done"], n - 3)
                cp(gate[:, q, :], slotin[:, q % 2, :, C]).then_inc(S["gate_done"], 1)
                cp(dest[:, q, :], slotin[:, q % 2, :, C + 1]).then_inc(S["dest_done"], 1)

            def finish(n, q, e):
                dve.wait_ge(S["y_mm"], n + 1)
                if earlier(n):
                    dve.wait_ge(S["y_done"], n)
                tt(ysum, ps[:, 4 + q % 2, :].rearrange("p (j c) -> p j c", j=NT),
                   b2_sb[:, bass.ds(e, 1), :].to_broadcast([P, NT, C]), ALU.add).then_inc(S["y_add"], 1)
                dve.wait_ge(S["y_add"], n + 1)
                dve.wait_ge(S["gate_done"], n + 1)
                if earlier(n, 2):
                    dve.wait_ge(S[f"picked{q % 2}"], 16 * NT * e)
                tt(yout[:, q % 2], ysum, gate[:, q, :].unsqueeze(2).to_broadcast([P, NT, C]), ALU.mult)\
                    .then_inc(S["y_done"], 1)

            dve.wait_ge(S["b_in"], 32)
            slots_copy(0, 0, 0)
            slots_copy(1, 1, 0)
            for n in range(4):
                slots_copy(n + 2, (n + 2) % 4, (n + 2) // 2)
                finish(n, n, n // 2)
            with dve.Fori(1, E // 2 - 1) as i:
                for q in range(4):
                    slots_copy(4 * i + q + 2, (q + 2) % 4, 2 * i + (q + 2) // 2)
                    finish(4 * i + q, q, 2 * i + q // 2)
            for n in range(2 * E - 4, 2 * E):
                if n + 2 < 2 * E:
                    slots_copy(n + 2, (n + 2) % 4, (n + 2) // 2)
                finish(n, n % 4, n // 2)

            for b in range(B):
                dve.wait_ge(two_in[b], 32)
                tt(two[:, b, 0], two[:, b, 0], two[:, b, 1], ALU.add).then_inc(S["two_sum"], 1)
                dve.wait_ge(S["two_sum"], b + 1)
                tt(two[:, b, 0], two[:, b, 0], modB[:, b:b + 1, 3 * C:4 * C].to_broadcast([P, NT, C]),
                   ALU.mult).then_inc(S["two_gb"], 1)

        @block.gpsimd
        def _(pool):
            sel_, tt, ts = nc.gpsimd.affine_select, nc.gpsimd.tensor_tensor, nc.gpsimd.tensor_scalar
            ms = nc.gpsimd.memset
            ms(ident[:, :], 0.0).then_inc(S["ident0"], 1)
            ms(identb[:, :], 0.0).then_inc(S["ident0"], 1)
            ms(mask[:, :, :], 0.0).then_inc(S["ident0"], 1)
            ms(upper[:, :], 1.0).then_inc(S["ident0"], 1)
            ms(empty[:, :], 0.0).then_inc(S["ident0"], 1)
            ms(onesb[:, :], 1.0).then_inc(S["consts"], 1)
            ms(vhalf[:, :], -0.5).then_inc(S["consts"], 1)
            ms(zeros[:, :], 0.0).then_inc(S["consts"], 1)
            pool.wait_ge(S["ident0"], 5)
            ms(empty[:, C + 1:C + 2], FAR).then_inc(S["consts"], 1)
            sel_(out=ident[:, :], in_=ident[:, :], compare_op=ALU.not_equal, fill=1.0, base=0,
                 pattern=[[-1, P]], channel_multiplier=1).then_inc(S["consts"], 1)
            sel_(out=identb[:, :], in_=identb[:, :], compare_op=ALU.not_equal, fill=1.0, base=0,
                 pattern=[[-1, P]], channel_multiplier=1).then_inc(S["consts"], 1)
            sel_(out=mask[:, :, :], in_=mask[:, :, :], compare_op=ALU.is_ge, fill=NEG, base=0,
                 pattern=[[0, 4], [-1, P]], channel_multiplier=1).then_inc(S["consts"], 1)
            sel_(out=upper[:, :], in_=upper[:, :], compare_op=ALU.is_gt, fill=0.0, base=0,
                 pattern=[[1, P]], channel_multiplier=-1).then_inc(S["consts"], 1)
            nc.gpsimd.iota(erev[:, :], [[-1, E]], base=E, channel_multiplier=0,
                           allow_small_or_imprecise_dtypes=True).then_inc(S["consts_b"], 1)
            nc.gpsimd.iota(eoff[:, :], [[CAP, E]], base=0, channel_multiplier=0,
                           allow_small_or_imprecise_dtypes=True).then_inc(S["consts_b"], 1)
            nc.gpsimd.iota(tokid[:, :, :], [[N, 2], [P, NT]], base=0, channel_multiplier=1,
                           allow_small_or_imprecise_dtypes=True).then_inc(S["id_next"], 1)

            def clear(z):
                ms(krows[:, z].bitcast(U32), 0).then_inc(S[f"clear{z}"], 1)

            def clear_values():
                ms(vpad[:, :, :, :, :], 0.0).then_inc(S["vclear"], 1)
                pool.wait_ge(S["vclear"], 1)
                vslot = vpad[:, :, :, :, :].rearrange("p a j (x i) c -> p (a j x) i c", i=2)
                for i in range(2):
                    ms(vslot[:, :, i, (D + 1) * i + D], 1.0).then_inc(S["vones"], 1)

            def prepare(b, u, s):
                if s == 6:
                    pool.wait_ge(S["s1_var"], b + 1)
                    ts(l1s[:, 2, :], l1s[:, 1, :], 1.0 / C, EPS, ALU.mult, ALU.add).then_inc(S["s1_v"], 1)
                if s == 7:
                    pool.wait_ge(S["s1_v"], b + 1)
                    if earlier(b):
                        pool.wait_ge(S["s1_norm"], b)
                    tt(l1s[:, 3, :], l1s[:, 2, :], vhalf[:, :], ALU.pow).then_inc(S["s1_rstd"], 1)
                for (z, z32, part, s1) in (("q", q32, qpart, 17), ("k", k32, kpart, 21)):
                    if s == s1:
                        pool.wait_ge(S[z + "1"], b + 1)
                        tt(z32[:, :], z32[:, :], part[:, 0, :], ALU.subtract).then_inc(S[z + "r"], 1)
                    if s == s1 + 3:
                        pool.wait_ge(S[z + "2"], b + 1)
                        if earlier(b):
                            pool.wait_ge(S["qk_stored"], 48 * b)
                        tt(part[:, 2, :], z32[:, :], part[:, 1, :], ALU.subtract).then_inc(S[z + "3"], 1)

            def place_values(b, par):
                if not earlier(b):
                    pool.wait_ge(S["vones"], 2)
                pool.wait_ge(S["v_copied"], b + 1)
                if earlier(b, 2):
                    pool.wait_ge(S["pved"], GB * (b - 1))
                dst = vpad[:, par].rearrange("p j (x i) c -> p (j x) i c", i=2)
                src = vtmp[:, :, :].rearrange("p j (x i d) -> p (j x) i d", i=2, d=D)
                for i in range(2):
                    last = nc.gpsimd.tensor_copy(dst[:, :, i, (D + 1) * i:(D + 1) * i + D], src[:, :, i, :])
                last.then_inc(S["v_placed"], 1)

            def causal(b, s):
                kind, pos, nh = UNITS[s % UH]
                w = width(kind)
                pool.wait_ge(S["expd"], UB * b + s + 1)
                blk = prob[:, s % PRING, 0:nh * w].rearrange("p (n w) -> p n w", n=nh)[:, :, 0:P]
                sel_(out=blk, in_=blk, compare_op=ALU.is_ge, fill=0.0, base=0,
                     pattern=[[0, nh], [1, P]], channel_multiplier=-1).then_inc(S["masked"], 1)

            def output(b, u, s):
                if s == 22:
                    pool.wait_ge(S["proj_ga"], b + 1)
                    tt(xall[:, b], proj[:, :, :], xall[:, b], ALU.add).then_inc(S["x1_done"], 1)
                if s == 30:
                    pool.wait_ge(S["s2_var"], b + 1)
                    ts(l2s[:, 2, :], l2s[:, 1, :], 1.0 / C, EPS, ALU.mult, ALU.add).then_inc(S["s2_v"], 1)
                if s == 31:
                    pool.wait_ge(S["s2_v"], b + 1)
                    if earlier(b):
                        pool.wait_ge(S["s2_norm"], b)
                    tt(l2s[:, 3, :], l2s[:, 2, :], vhalf[:, :], ALU.pow).then_inc(S["s2_rstd"], 1)
                if s == 33:
                    pool.wait_ge(S["s2_norm"], b + 1)
                    if earlier(b):
                        pool.wait_ge(S["h2_b"], b)
                    tt(h2[:, :, :], l2[:, :, :], modB[:, bass.ds(b, 1), 2 * C:3 * C].to_broadcast([P, NT, C]),
                       ALU.mult).then_inc(S["h2_a"], 1)
                if s == 35:
                    pool.wait_ge(S["h2_a"], b + 1)
                    if earlier(b, 2):
                        pool.wait_ge(S["scattered"], 16 * 2 * NT * (b - 1))
                        pool.wait_ge(S["h2T_tr"], b)
                        pool.wait_ge(S["rows_b"], b)
                    tt(rows[:, u, 0, :, 0:C], h2[:, :, :],
                       modB[:, bass.ds(b, 1), C:2 * C].to_broadcast([P, NT, C]), ALU.add).then_inc(S["h2_b"], 1)

            def route(b, u, s):
                if s == 12:
                    pool.wait_ge(S["id_next"], b + 1)
                    if earlier(b):
                        pool.wait_ge(S["scattered"], 16 * 2 * NT * b)
                    nc.gpsimd.tensor_copy(rows[:, u, :, :, C + 1], tokid[:, :, :]).then_inc(S["id_set"], 1)
                if s == 14:
                    pool.wait_ge(S["id_set"], b + 1)
                    ts(tokid[:, :, :], tokid[:, :, :], float(T), None, ALU.add).then_inc(S["id_next"], 1)
                if s == 26:
                    pool.wait_ge(S["r_index"], b + 1)
                    pool.wait_ge(S["g_two"], b + 1)
                    pool.wait_ge(S["rows_b"], b + 1)
                    pool.wait_ge(S["prefilled"], 32)
                if s >= 26 and s < 42 and s % 2 == 0:
                    k, j = divmod((s - 26) // 2, NT)
                    pool.indirect_dma_start(slots, bass.IndirectOffsetOnAxis(index[:, u, k, j:j + 1], 0),
                                            rows[:, u, k, j, :], None, bounds_check=E * CAP - 1,
                                            oob_is_err=False).then_inc(S["scattered"], 16)

            def step(t, u):
                for s in range(UB):
                    if isinstance(t, int) and t == -2:
                        if s == 8:
                            clear(0)
                        if s == 26:
                            clear_values()
                            clear(1)
                    if begun(t):
                        causal(t, s)
                    if s == 5 and begun(t + 1):
                        place_values(t + 1, 1 - u)
                    if begun(t + 2):
                        prepare(t + 2, u, s)
                    if begun(t - 1):
                        output(t - 1, 1 - u, s)
                    if begun(t - 2):
                        route(t - 2, u, s)

            timeline(pool, step)

            def send(n, q):
                pool.wait_ge(S["y_done"], n + 1)
                for j in range(NT):
                    pool.indirect_dma_start(picks, bass.IndirectOffsetOnAxis(dest[:, q, j:j + 1], 0),
                                            yout[:, q % 2, j, :], None, bounds_check=2 * N - 1,
                                            oob_is_err=False).then_inc(S[f"picked{q % 2}"], 16)

            for n in range(2 * E):
                send(n, n % 4)

            with pool.Fori(0, B) as b:
                pool.wait_ge(S["two_gb"], b + 1)
                tt(xall[:, b], xall[:, b], two[:, b, 0], ALU.add).then_inc(S["x2_done"], 1)


def kernel(L0_attn_x, L0_attn_Q, L0_attn_K, L0_attn_V, L0_attn_O, L0_ffn_Wr, L0_ffn_br, L0_ffn_W1,
           L0_ffn_b1, L0_ffn_W2, L0_ffn_b2, L0_c, L0_wmod):
    import numpy as np
    import concourse.bacc as bacc
    from concourse.bass_utils import run_bass_kernel_spmd

    heads = [half * HH + h for half in range(HALVES) for h in ORDER]

    def by_position(w):
        return np.asarray(w)[:, heads, :].transpose(0, 2, 1).reshape(C, C)

    arrays = {
        "x": L0_attn_x,
        "wq": by_position(L0_attn_Q),
        "wk": by_position(L0_attn_K),
        "wv": np.asarray(L0_attn_V).reshape(C, C),
        "wo": L0_attn_O,
        "wr": L0_ffn_Wr,
        "br": L0_ffn_br,
        "w1": L0_ffn_W1,
        "b1": np.asarray(L0_ffn_b1).reshape(E * NF, P).transpose(1, 0),
        "w2": L0_ffn_W2,
        "b2": L0_ffn_b2,
        "cT": np.asarray(L0_c).transpose(1, 0),
        "wmod": L0_wmod,
    }
    arrays = {"in_" + n: np.ascontiguousarray(a) for n, a in arrays.items()}
    nc = bacc.Bacc("TRN2", target_bir_lowering=False, num_devices=1)
    aps = [nc.dram_tensor(n, a.shape, mybir.dt.from_np(a.dtype), kind="ExternalInput").ap()
           for n, a in arrays.items()]
    out = nc.dram_tensor("out_0", (B, T, C), F32, kind="ExternalOutput").ap()
    adaln_moe_kernel(nc, *aps, out)
    r = run_bass_kernel_spmd(nc, [arrays], core_ids=[0])
    return r.results[0]["out_0"]
```

```python
from contextlib import ExitStack

import concourse.bass as bass
from concourse import mybir

F32 = mybir.dt.float32
BF16 = mybir.dt.bfloat16
U32 = mybir.dt.uint32
ALU = mybir.AluOpType
ACT = mybir.ActivationFunctionType
AX = mybir.AxisListType

P = 128
B, T, C, H = 8, 512, 128, 16
D = C // H
NT = T // P
N = B * T
E = 8
FF = 512
NF = FF // P
CAP = N * 2 // E
ROW = C + 2
FAR = 1.0e6
NEG = -3.0e38
EPS = 1e-5
SCALE = float(D) ** 0.5

HALVES = 2
HH = H // HALVES
ORDER = [0, 2, 4, 6, 1, 3, 5, 7]
PARTS = 3
QROWS = PARTS * D
SROWS = 96
MROW = 96

UNITS = ([(0, p, 1) for p in range(8)] + [(1, p, 1) for p in range(8)]
         + [(2, p, 2) for p in range(0, 8, 2)] + [(3, p, 4) for p in range(0, 8, 4)])
UH = len(UNITS)
UB = HALVES * UH
GROUPS = [range(0, 4), range(4, 8), range(8, 12), range(12, 16), range(16, 20), range(20, 22)]
GB = HALVES * len(GROUPS)
AT = {7: 0, 11: 1, 15: 2, 19: 3, 1: 4, 3: 5}
SRING = 3
PRING = UH // 2


def width(kind):
    return T - P * kind


def group_of(u):
    return [n for n, g in enumerate(GROUPS) if u in g][0]


def sbank(s):
    return s % SRING if s < UB - UB % SRING else s - (UB - UB % SRING)


def sbank_before(s):
    for back in range(1, UB):
        if sbank((s - back) % UB) == sbank(s):
            return (1, s - back + UB) if s < back else (0, s - back)


def adaln_moe_kernel(nc, x, wq, wk, wv, wo, wr, br, w1, b1, w2, b2, cT, wmod, out):
    ctx = ExitStack()
    with ctx:
        def sb(name, shape, dt=F32):
            return ctx.enter_context(nc.sbuf_tensor(name, shape, dt))

        def sem(name):
            return ctx.enter_context(nc.semaphore(name))

        qd = nc.dram_tensor("q_parts_dram", [QROWS, H, T], BF16).ap()
        kd = nc.dram_tensor("k_parts_dram", [5 * D, H, T], BF16).ap()
        modd = nc.dram_tensor("mod_dram", [B, 4 * C], F32).ap()
        slots = nc.dram_tensor("slots_dram", [E * CAP, ROW], F32).ap()
        picks = nc.dram_tensor("picks_dram", [2 * N, C], F32).ap()

        xall = sb("xall", [P, B, NT, C])
        modB = sb("modB", [P, B, 4 * C])
        qrows = sb("qrows", [P, 2, H, T], BF16)
        krows = sb("krows", [P, 2, H, T], BF16)
        prob = sb("prob", [P, PRING, T])
        vpad = sb("vpad", [P, 2, NT, H, 32])
        wq_sb = sb("wq_sb", [P, C])
        wk_sb = sb("wk_sb", [P, C])
        wv_sb = sb("wv_sb", [P, C])
        wo_sb = sb("wo_sb", [P, C])
        wr_sb = sb("wr_sb", [P, E])
        br_sb = sb("br_sb", [P, E])
        b1_sb = sb("b1_sb", [P, E * NF])
        b2_sb = sb("b2_sb", [P, E, C])
        w1_sb = sb("w1_sb", [P, 2, FF])
        w2_sb = sb("w2_sb", [P, 2, NF, C])
        cT_sb = sb("cT_sb", [P, B])
        csig = sb("csig", [P, B])
        csilu = sb("csilu", [P, B])
        saT = sb("saT", [P, B])
        caT = sb("caT", [P, B])
        wmod_sb = prob[:, 0:2].rearrange("p a t -> p (a t)")[:, 0:6 * C]
        mrow = prob[0:B, 2]
        msgn = prob[0:B, 3]
        ident = sb("ident", [P, P])
        identb = sb("identb", [P, P], BF16)
        mask = sb("mask", [P, 4, P], BF16)
        upper = sb("upper", [P, P], BF16)
        onesb = sb("onesb", [P, P], BF16)
        erev = sb("erev", [P, E])
        eoff = sb("eoff", [P, E])
        tokid = sb("tokid", [P, 2, NT])
        vhalf = sb("vhalf", [P, NT])
        empty = sb("empty", [P, ROW])
        zeros = sb("zeros", [P, T])
        l1 = sb("ln1", [P, NT, C])
        l1q = sb("ln1_square", [P, NT, C])
        l1s = sb("ln1_sum", [P, 4, NT])
        l2 = sb("ln2", [P, NT, C])
        l2q = sb("ln2_square", [P, NT, C])
        l2s = sb("ln2_sum", [P, 4, NT])
        h1T = sb("h1T", [P, T])
        q32 = sb("q32", [P, T])
        k32 = sb("k32", [P, T])
        qpart = sb("qpart", [P, PARTS, T], BF16)
        kpart = sb("kpart", [P, PARTS, T], BF16)
        vtmp = sb("vtmp", [P, NT, C])
        negmax = sb("negmax", [P, 2, 4, HH])
        negrest = sb("negrest", [P, 2, 4, HH])
        mparts = sb("mparts", [P, 2, 4, PARTS, HH], BF16)
        mT = sb("mT", [PARTS * HH, 2, T], BF16)
        oS = sb("oS", [P, 2, T])
        rsum = sb("rsum", [P, 2, 16, 2])
        on = sb("on", [P, NT, C])
        oT = sb("oT", [P, T])
        wo_ga = sb("wo_ga", [P, C])
        h2 = sb("h2", [P, NT, C])
        rows = sb("rows", [P, 2, 2, NT, ROW])
        h2T = sb("h2T", [P, T])
        lg = sb("lg", [P, NT, E])
        lg2 = sb("lg2", [P, NT, E])
        top = sb("top", [P, 2, NT])
        eq = sb("eq", [P, NT, E])
        pick = sb("pick", [P, NT, E])
        best = sb("best", [P, 2, NT])
        swap = sb("swap", [P, NT])
        hot = sb("hot", [P, 2, NT, E])
        sel = sb("sel", [P, NT, E], BF16)
        gap = sb("gap", [P, NT])
        gexp = sb("gexp", [P, NT])
        gden = sb("gden", [P, NT])
        rank = sb("rank", [P, NT, E])
        slot = sb("slot", [P, NT, E])
        carry = sb("carry", [P, E])
        prod = sb("prod", [P, 2, NT, E])
        prod2 = sb("prod2", [P, 2, NT, E])
        myrank = sb("myrank", [P, 2, NT])
        myslot = sb("myslot", [P, 2, NT])
        over = sb("over", [P, 2, NT])
        index = sb("index", [P, 2, 2, NT], U32)
        qf = qrows[:, :, :, :].rearrange("p a h t -> p (a h t)").bitcast(F32)
        kf = krows[:, :, :, :].rearrange("p a h t -> p (a h t)").bitcast(F32)
        hid = qf[:, 0:2 * NF * T].rearrange("p (a k t) -> p a k t", a=2, k=NF)
        slotT = qf[:, 4096:4096 + 2 * T].rearrange("p (a t) -> p a t", a=2)
        ysum = qf[:, 5120:5120 + T].rearrange("p (j c) -> p j c", j=NT)
        yout = qf[:, 5632:5632 + 2 * T].rearrange("p (a j c) -> p a j c", a=2, j=NT)
        two = kf.rearrange("p (b k j c) -> p b k j c", b=B, k=2, j=NT)
        slotin = qf[:, 6656:6656 + 2 * NT * ROW].rearrange("p (a j c) -> p a j c", a=2, j=NT)
        gate = sb("gate", [P, 4, NT])
        dest = sb("dest", [P, 4, NT], U32)

        ps = ctx.enter_context(nc.psum_tensor("ps", [P, 8, T], F32))
        SB_, TB, OB, M0, M1 = 0, SRING, 5, 6, 7
        m1b = ps[:, M1, :].bitcast(BF16)

        names = """x0_in x_in wqkv_in wo_in mod_w_in route_w_in b_in prefilled mod_stored modB_in
        c_exp c_one c_rec c_silu modT_mm modrow_mm mod_T mod_row mod_sgn mod_sgn1 mod_abs mod_max mod_out
        consts ident0 consts_b carry0 clear0 clear1 cleared0 cleared1 vclear vones
        s1_sum s1_cen s1_var s1_v s1_rstd s1_norm s1_tr h1_ready
        q_mm k_mm v_mm v_copied q1 q2 q3 qr k1 k2 k3 kr v_placed
        qk_stored half0_loaded half1_loaded
        scored maxed n1 nr n2 n3 m_tr m_copied mrow0_in mrow1_in
        shifted expd masked pved o_copied o_tr o_rec o_norm oT_tr oT_copied proj_mm wo_ga x1_done
        s2_sum s2_cen s2_var s2_v s2_rstd s2_norm h2_a h2_b rows_b h2T_tr h2T_copied logit_mm
        r_log r_top1 r_eq1 r_pick1 r_best1 r_swap r_hot1 r_log2 r_top2 r_eq2 r_pick2 r_best2 r_hot2 r_sel
        g_gap g_exp g_den g_one g_two id_set rank_mm r_rank r_carry r_slot r_prod r_prod2 r_myrank r_myslot
        r_over r_index scattered0 scattered1 id_next table_in
        w_in0 w_in1 slot_in0 slot_in1 slot_tr slot_T hid_mm hid_done y_mm y_add y_done gate_done dest_done picked0 picked1
        two_gb x2_even x2_odd out_done""".split()
        S = {n: sem(n) for n in names}
        two_in = [sem(f"two_in{b}") for b in range(B)]
        low_in = [sem(f"low_in{b}") for b in range(0, B, 4)]

        block = ctx.enter_context(nc.Block())

        def begun(b):
            return 0 <= b < B

        def earlier(b, back=1):
            return not isinstance(b, int) or b >= back

        def timeline(eng, step):
            for t in range(-2, B + 2):
                step(t, t % 2)

        @block.sync
        def _(sp):
            sp.dma_start(xall[:, 0], x[0].rearrange("(j p) c -> p j c", p=P)).then_inc(S["x0_in"], 16)
            sp.dma_start(cT_sb[:, :], cT).then_inc(S["mod_w_in"], 16)
            sp.dma_start(wmod_sb, wmod).then_inc(S["mod_w_in"], 16)
            sp.dma_start(wq_sb[:, :], wq).then_inc(S["wqkv_in"], 16)
            sp.dma_start(wk_sb[:, :], wk).then_inc(S["wqkv_in"], 16)
            sp.dma_start(wv_sb[:, :], wv).then_inc(S["wqkv_in"], 16)
            sp.dma_start(xall[:, 1:B], x[1:B].rearrange("b (j p) c -> p b j c", p=P)).then_inc(S["x_in"], 16)
            sp.dma_start(wo_sb[:, :], wo).then_inc(S["wo_in"], 16)
            sp.dma_start(wr_sb[:, :], wr).then_inc(S["route_w_in"], 16)
            sp.dma_start(br_sb[:, :], br.partition_broadcast(P)).then_inc(S["route_w_in"], 16)
            sp.dma_start(b1_sb[:, :], b1).then_inc(S["b_in"], 16)
            sp.dma_start(b2_sb[:, :, :], b2.partition_broadcast(P)).then_inc(S["b_in"], 16)
            sp.wait_ge(S["mod_out"], 3)
            sp.dma_start(modd, mrow).then_inc(S["mod_stored"], 16)
            sp.wait_ge(S["mod_stored"], 16)
            sp.dma_start(modB[:, :, :], modd.partition_broadcast(P)).then_inc(S["modB_in"], 16)
            for z in range(2):
                sp.wait_ge(S[f"clear{z}"], 2)
                sp.dma_start(krows[MROW:MROW + PARTS, z].rearrange("p h (n m) -> p (h n) m", m=P),
                             onesb[0:PARTS, None, :].to_broadcast([PARTS, H * NT, P]))\
                  .then_inc(S[f"cleared{z}"], 16)

            def prefill(t):
                if t == 0:
                    sp.dma_start(slots.rearrange("(p n) c -> p n c", p=P),
                                 empty[:, None, :].to_broadcast([P, E * CAP // P, ROW])).then_inc(S["prefilled"], 16)
                if t == 1:
                    sp.dma_start(picks.rearrange("(p n m) c -> p n (m c)", p=P, m=T // C),
                                 zeros[:, None, :].to_broadcast([P, 2 * N // P // 4, T])).then_inc(S["prefilled"], 16)

            def load_rows(b, par, half):
                heads = slice(half * HH, (half + 1) * HH)
                done = S["half0_loaded" if half == 0 else "half1_loaded"]
                for j in range(PARTS):
                    r = slice(j * QROWS, (j + 1) * QROWS)
                    sp.dma_start(qrows[r, par, heads], qd[:, heads]).then_inc(done, 16)
                    sp.dma_start(krows[r, par, heads], kd[j * D:j * D + QROWS, heads]).then_inc(done, 16)

            def load_maxima(b, par, half):
                heads = slice(half * HH, (half + 1) * HH)
                sp.wait_ge(S["m_copied"], 2 * b + half + 1)
                for i in range(PARTS):
                    sp.dma_start(qrows[MROW + i:MROW + i + 1, par, heads],
                                 mT[i * HH:(i + 1) * HH, half]).then_inc(S[f"mrow{half}_in"], 16)

            def step(t, u):
                prep, att = t + 2, t
                if begun(att):
                    load_maxima(att, u, 1)
                prefill(t)
                if begun(prep):
                    if earlier(prep):
                        sp.wait_ge(S["half0_loaded"], 96 * prep)
                        sp.wait_ge(S["half1_loaded"], 96 * prep)
                    sp.wait_ge(S["q3"], prep + 1)
                    sp.dma_start(qd.rearrange("(a d) h t -> (d h) a t", a=PARTS), qpart[:, :, :])\
                      .then_inc(S["qk_stored"], 16)
                    sp.wait_ge(S["k3"], prep + 1)
                    sp.dma_start(kd[0:QROWS].rearrange("(a d) h t -> (d h) a t", a=PARTS), kpart[:, :, :])\
                      .then_inc(S["qk_stored"], 16)
                    sp.dma_start(kd[QROWS:5 * D].rearrange("(a d) h t -> (d h) a t", a=2), kpart[:, 0:2, :])\
                      .then_inc(S["qk_stored"], 16)
                    sp.wait_ge(S["qk_stored"], 48 * (prep + 1))
                    if not earlier(prep, 2):
                        sp.wait_ge(S[f"clear{u}"], 2)
                    if begun(att):
                        sp.wait_ge(S["shifted"], UB * att + UH)
                    load_rows(prep, u, 0)
                if begun(t + 1):
                    load_maxima(t + 1, 1 - u, 0)
                if begun(prep):
                    if begun(att):
                        sp.wait_ge(S["shifted"], UB * att + UB)
                    load_rows(prep, u, 1)

            timeline(sp, step)

            def load_slots(n, q):
                if earlier(n, 2):
                    sp.wait_ge(S["slot_tr"], n - 1)
                    sp.wait_ge(S["dest_done"], n - 1)
                sp.dma_start(slotin[:, q % 2], slots[bass.ds(n * T, T), :].rearrange("(j p) c -> p j c", p=P))\
                  .then_inc(S[f"slot_in{q % 2}"], 16)

            def load_expert(e, par):
                if earlier(e, 2):
                    sp.wait_ge(S["y_mm"], 2 * e - 2)
                sp.dma_start(w1_sb[:, par], w1[e]).then_inc(S[f"w_in{par}"], 16)
                sp.dma_start(w2_sb[:, par], w2[e].rearrange("(k p) c -> p k c", p=P)).then_inc(S[f"w_in{par}"], 16)

            load_expert(0, 0)
            load_expert(1, 1)
            for par in range(2):
                sp.wait_ge(S[f"scattered{par}"], 16 * 2 * NT * (B // 2))
            for n in range(4):
                load_slots(n, n)
            with sp.Fori(1, E // 2) as i:
                for q in range(4):
                    load_slots(4 * i + q, q)
                    if q % 2 == 0:
                        load_expert(2 * i + q // 2, q // 2)

            pv = picks.rearrange("(k b j p) c -> b k p j c", k=2, b=B, p=P)
            for k, e in ((0, E - 1), (1, E)):
                for par in range(2):
                    sp.wait_ge(S[f"picked{par}"], 16 * NT * e)
                for b in range(B):
                    sp.dma_start(two[:, b, k], pv[b, k]).then_inc(two_in[b] if k else low_in[b // 4], 16)
            for b in range(B):
                sp.wait_ge(S["x2_odd" if b % 2 else "x2_even"], B // 2 + b // 2 + 1)
                sp.dma_start(out[b].rearrange("(j p) c -> p j c", p=P), xall[:, b]).then_inc(S["out_done"], 16)
            sp.wait_ge(S["out_done"], 16 * B)

        @block.tensor
        def _(pe):
            mm = nc.tensor.matmul
            pe.wait_ge(S["mod_w_in"], 32)
            pe.wait_ge(S["c_silu"], 1)
            for j in range(2):
                last = mm(ps[:, M0, j * B:(j + 1) * B], wmod_sb[:, j * C:(j + 1) * C], csilu[:, :],
                          start=True, stop=True)
            last.then_inc(S["modT_mm"], 1)
            mm(ps[0:B, M1, :], csilu[:, :], wmod_sb[:, 2 * C:6 * C], start=True, stop=True)\
                .then_inc(S["modrow_mm"], 1)
            pe.wait_ge(S["consts"], 8)
            pe.wait_ge(S["wqkv_in"], 48)
            pe.wait_ge(S["mod_T"], 2)
            pe.wait_ge(S["mod_row"], 1)

            def prepare(b, u, s):
                if s == 13:
                    pe.wait_ge(S["s1_norm"], NT * (b + 1))
                    if begun(b - 2):
                        pe.wait_ge(S["m_copied"], 2 * b - 2)
                    elif earlier(b):
                        pe.wait_ge(S["v_copied"], b)
                    for j in range(NT):
                        last = nc.tensor.transpose(ps[:, M1, j * P:(j + 1) * P], l1[:, j, :], ident[:, :])
                    last.then_inc(S["s1_tr"], 1)
                if s == 16:
                    pe.wait_ge(S["h1_ready"], b + 1)
                    mm(ps[:, M1, :], wq_sb[:, :], h1T[:, :], start=True, stop=True).then_inc(S["q_mm"], 1)
                if s == 20:
                    pe.wait_ge(S["qr"], b + 1)
                    mm(ps[:, M1, :], wk_sb[:, :], h1T[:, :], start=True, stop=True).then_inc(S["k_mm"], 1)
                if s == 24:
                    pe.wait_ge(S["kr"], b + 1)
                    for j in range(NT):
                        last = mm(ps[:, M1, j * P:(j + 1) * P], h1T[:, j * P:(j + 1) * P], wv_sb[:, :],
                                  start=True, stop=True)
                    last.then_inc(S["v_mm"], 1)

            def maxima_T(b, half):
                pe.wait_ge(S["n3"], 2 * b + half + 1)
                for j in range(NT):
                    last = nc.tensor.transpose(m1b[0:PARTS * HH, j * P:(j + 1) * P],
                                               mparts[:, half, j].rearrange("p a h -> p (a h)"), identb[:, :])
                last.then_inc(S["m_tr"], 1)

            def score(b, u, s):
                half, (kind, pos, nh) = s // UH, UNITS[s % UH]
                qb = NT - 1 - kind
                w = width(kind)
                if s % UH == 0:
                    pe.wait_ge(S[f"half{half}_loaded"], 96 * (b + 1))
                back, before = sbank_before(s)
                if not back or earlier(b):
                    pe.wait_ge(S["maxed"], UB * (b - back) + before + 1)
                bank = ps[:, SB_ + sbank(s), :]
                for i in range(nh):
                    h = half * HH + pos + i
                    mm(bank[:, i * w:(i + 1) * w], qrows[0:SROWS, u, h, qb * P:(qb + 1) * P],
                       krows[0:SROWS, u, h, 0:w], start=(i == 0), stop=False, skip_group_check=True)
                diag = bank[:, 0:nh * w].rearrange("p (n w) -> p n w", n=nh)[:, :, qb * P:w]
                mm(diag, identb[:, :], mask[:, 0:nh, :], start=False, stop=True,
                   skip_group_check=True).then_inc(S["scored"], 1)

            def shifted(b, u, s):
                half, (kind, pos, nh) = s // UH, UNITS[s % UH]
                w = width(kind)
                if s % UH == 0:
                    pe.wait_ge(S[f"mrow{half}_in"], 48 * (b + 1))
                    if not earlier(b, 2):
                        pe.wait_ge(S[f"cleared{b % 2}"], 16)
                if s >= 2 or earlier(b):
                    pe.wait_ge(S["expd"], UB * b + s - 1)
                bank = ps[:, TB + s % 2, :]
                for i in range(nh):
                    h = half * HH + pos + i
                    last = mm(bank[:, i * w:(i + 1) * w], krows[:, u, h, kind * P:(kind + 1) * P],
                              qrows[:, u, h, kind * P:T], start=True, stop=True)
                last.then_inc(S["shifted"], 1)

            def values(b, u, half, g):
                if g == 0:
                    if half == 0:
                        pe.wait_ge(S["v_placed"], b + 1)
                    if half or earlier(b):
                        pe.wait_ge(S["o_copied"], 2 * b + half)
                pe.wait_ge(S["masked"], UB * b + UH * half + GROUPS[g][-1] + 1)
                for v in GROUPS[g]:
                    kind, pos, nh = UNITS[v]
                    w = width(kind)
                    for i in range(nh):
                        grp, slt = (pos + i) % 4, (pos + i) // 4
                        head = half * HH + ORDER[pos + i]
                        last = mm(ps[32 * grp:32 * grp + 32, OB, kind * P:T], vpad[:, u, kind, head, :],
                                  prob[:, (half * UH + v) % PRING, i * w:(i + 1) * w],
                                  start=(kind == 0 and slt == 0), stop=(kind == 3 and slt == 1),
                                  skip_group_check=True)
                last.then_inc(S["pved"], 1)

            def sums_T(b, half):
                pe.wait_ge(S["o_copied"], 2 * b + half + 1)
                for j in range(NT):
                    last = nc.tensor.transpose(ps[:, M0, j * P:(j + 1) * P], oS[:, half, j * P:(j + 1) * P],
                                               ident[:, :])
                last.then_inc(S["o_tr"], 1)

            def output(b, u, s):
                if s == 8:
                    if earlier(b):
                        pe.wait_ge(S["r_log"], b)
                    pe.wait_ge(S["o_norm"], 4 * b + 2)
                    sums_T(b, 1)
                if s == 14:
                    pe.wait_ge(S["o_norm"], 4 * b + 4)
                    for j in range(NT):
                        last = nc.tensor.transpose(ps[:, M0, j * P:(j + 1) * P], on[:, j, :], ident[:, :])
                    last.then_inc(S["oT_tr"], 1)
                if s == 20:
                    pe.wait_ge(S["wo_ga"], b + 1)
                    pe.wait_ge(S["oT_copied"], b + 1)
                    if earlier(b):
                        pe.wait_ge(S["r_carry"], b)
                    for j in range(NT):
                        last = mm(ps[:, M0, j * P:(j + 1) * P], oT[:, j * P:(j + 1) * P], wo_ga[:, :],
                                  start=True, stop=True)
                    last.then_inc(S["proj_mm"], 1)

            def route(b, u, s):
                if s == 1:
                    pe.wait_ge(S["h2_b"], b + 1)
                    if begun(b + 1):
                        pe.wait_ge(S["o_norm"], 4 * b + 6)
                    for j in range(NT):
                        last = nc.tensor.transpose(ps[:, M0, j * P:(j + 1) * P], rows[:, u, 0, j, 0:C],
                                                   ident[:, :])
                    last.then_inc(S["h2T_tr"], 1)
                if s == 4:
                    if not earlier(b):
                        pe.wait_ge(S["route_w_in"], 32)
                    pe.wait_ge(S["h2T_copied"], b + 1)
                    for j in range(NT):
                        last = mm(ps[:, M0, j * E:(j + 1) * E], h2T[:, j * P:(j + 1) * P], wr_sb[:, :],
                                  start=True, stop=True)
                    last.then_inc(S["logit_mm"], 1)
                if s == 16:
                    pe.wait_ge(S["r_sel"], b + 1)
                    pe.wait_ge(S["r_log"], b + 1)
                    if begun(b + 1):
                        pe.wait_ge(S["oT_copied"], b + 2)
                    for j in range(NT + 1):
                        reg = ps[:, M0, j * E:(j + 1) * E]
                        for k in range(j):
                            last = mm(reg, onesb[:, :], sel[:, k, :], start=(k == 0), stop=(j == NT and k == j - 1))
                        if j < NT:
                            last = mm(reg, upper[:, :], sel[:, j, :], start=(j == 0), stop=True)
                    last.then_inc(S["rank_mm"], 1)

            def step(t, u):
                for s in range(UB):
                    if begun(t + 2):
                        prepare(t + 2, u, s)
                    if begun(t - 1):
                        output(t - 1, 1 - u, s)
                    if begun(t - 2):
                        route(t - 2, u, s)
                    if s == 9 and begun(t):
                        pe.wait_ge(S["m_copied"], 2 * t + 1)
                        maxima_T(t, 1)
                    if s == 30 and begun(t):
                        if begun(t - 1):
                            pe.wait_ge(S["x1_done"], t)
                        sums_T(t, 0)
                    if s == 31 and begun(t + 1):
                        if begun(t + 2):
                            pe.wait_ge(S["v_copied"], t + 3)
                        else:
                            pe.wait_ge(S["m_copied"], 2 * t + 2)
                        maxima_T(t + 1, 0)
                    if begun(t + 1):
                        score(t + 1, 1 - u, s)
                    if begun(t):
                        shifted(t, u, s)
                    half, v = divmod(s, UH)
                    if v in AT:
                        g = AT[v]
                        if g < 4 and begun(t):
                            values(t, u, half, g)
                        if g >= 4 and half == 1 and begun(t):
                            values(t, u, 0, g)
                        if g >= 4 and half == 0 and begun(t - 1):
                            values(t - 1, 1 - u, 1, g)

            timeline(pe, step)

            def up(n, q, pair):
                if q % 2 == 0:
                    pe.wait_ge(S[f"w_in{q // 2}"], 32 * (pair + 1))
                pe.wait_ge(S["slot_T"], n + 1)
                for k in range(NF):
                    if earlier(n):
                        pe.wait_ge(S["hid_done"], NF * (n - 1) + k + 1)
                    mm(ps[:, k, :], w1_sb[:, q // 2, k * P:(k + 1) * P], slotT[:, q % 2, :],
                       start=True, stop=True).then_inc(S["hid_mm"], 1)

            def slots_T(n, q, e):
                pe.wait_ge(S[f"slot_in{q % 2}"], 16 * (e + 1))
                if earlier(n):
                    pe.wait_ge(S["slot_T"], n)
                for j in range(NT):
                    last = nc.tensor.transpose(ps[:, 6, j * P:(j + 1) * P], slotin[:, q % 2, j, 0:C], ident[:, :])
                last.then_inc(S["slot_tr"], 1)

            def down(n, q, e):
                pe.wait_ge(S["hid_done"], NF * (n + 1))
                if earlier(n, 2):
                    pe.wait_ge(S["y_add"], n - 1)
                for j in range(NT):
                    for k in range(NF):
                        last = mm(ps[:, 4 + q % 2, j * P:(j + 1) * P], hid[:, q % 2, k, j * P:(j + 1) * P],
                                  w2_sb[:, q // 2, k, :], start=(k == 0), stop=(k == NF - 1))
                last.then_inc(S["y_mm"], 1)

            pe.wait_ge(S["r_carry"], B)
            pe.wait_ge(S["maxed"], UB * B)
            pe.wait_ge(S["expd"], UB * B)
            pe.wait_ge(S["o_copied"], 2 * B)
            slots_T(0, 0, 0)
            slots_T(1, 1, 0)
            up(0, 0, 0)
            for n in range(4):
                up(n + 1, (n + 1) % 4, (n + 1) // 4)
                slots_T(n + 2, (n + 2) % 4, (n + 2) // 2)
                down(n, n, n // 2)
            with pe.Fori(1, E // 2 - 1) as i:
                for q in range(4):
                    up(4 * i + q + 1, (q + 1) % 4, i + (q + 1) // 4)
                    slots_T(4 * i + q + 2, (q + 2) % 4, 2 * i + (q + 2) // 2)
                    down(4 * i + q, q, 2 * i + q // 2)
            for n in range(2 * E - 4, 2 * E):
                if n + 1 < 2 * E:
                    up(n + 1, (n + 1) % 4, (n + 1) // 4)
                if n + 2 < 2 * E:
                    slots_T(n + 2, (n + 2) % 4, (n + 2) // 2)
                down(n, n % 4, n // 2)

        @block.scalar
        def _(act):
            fn = nc.scalar.activation
            act.wait_ge(S["mod_w_in"], 32)
            fn(csig[:, :], cT_sb[:, :], ACT.Exp, scale=-1.0).then_inc(S["c_exp"], 1)
            act.wait_ge(S["modrow_mm"], 1)
            fn(mrow, ps[0:B, M1, :], ACT.Copy).then_inc(S["mod_row"], 1)
            act.wait_ge(S["mod_T"], 2)

            def prepare(b, u, s):
                if s in (3, 4):
                    act.wait_ge(S["s1_cen"], b + 1)
                    if earlier(b):
                        act.wait_ge(S["s1_v"], b)
                        act.wait_ge(S["s1_var"], NT * b)
                    for j in range(2 * (s - 3), 2 * (s - 3) + 2):
                        fn(l1q[:, j, :], l1[:, j, :], ACT.Square, accum_out=l1s[:, 1, j:j + 1]).then_inc(S["s1_var"], 1)
                if s in (9, 10):
                    act.wait_ge(S["s1_rstd"], b + 1)
                    for j in range(2 * (s - 9), 2 * (s - 9) + 2):
                        fn(l1[:, j, :], l1[:, j, :], ACT.Copy, scale=l1s[:, 3, j:j + 1]).then_inc(S["s1_norm"], 1)
                if s == 14:
                    act.wait_ge(S["s1_tr"], b + 1)
                    fn(h1T[:, :], ps[:, M1, :], ACT.Identity, bias=saT[:, bass.ds(b, 1)],
                       scale=caT[:, bass.ds(b, 1)]).then_inc(S["h1_ready"], 1)
                for (z, z32, part, s1) in (("q", q32, qpart, 17), ("k", k32, kpart, 21)):
                    if s == s1:
                        act.wait_ge(S[z + "_mm"], b + 1)
                        if earlier(b):
                            act.wait_ge(S["qk_stored"], 48 * b)
                        fn(part[:, 0, :], ps[:, M1, :], ACT.Copy).then_inc(S[z + "1"], 1)
                    if s == s1 + 3:
                        act.wait_ge(S[z + "r"], b + 1)
                        if earlier(b):
                            act.wait_ge(S["qk_stored"], 48 * b)
                        fn(part[:, 1, :], z32[:, :], ACT.Copy).then_inc(S[z + "2"], 1)
                if s == 25:
                    act.wait_ge(S["v_mm"], b + 1)
                    if earlier(b):
                        act.wait_ge(S["v_placed"], b)
                    fn(vtmp[:, :, :], ps[:, M1, :].rearrange("p (j c) -> p j c", j=NT), ACT.Copy)\
                        .then_inc(S["v_copied"], 1)

            def copy_maxima(b, half):
                act.wait_ge(S["m_tr"], 2 * b + half + 1)
                if earlier(b):
                    act.wait_ge(S[f"mrow{half}_in"], 48 * b)
                fn(mT[:, half, :], m1b[0:PARTS * HH, 0:T], ACT.Copy).then_inc(S["m_copied"], 1)

            def exps(b, u, s):
                half, (kind, pos, nh) = s // UH, UNITS[s % UH]
                w = nh * width(kind)
                if s == 0 and not earlier(b):
                    act.wait_ge(S["mod_stored"], 16)
                act.wait_ge(S["shifted"], UB * b + s + 1)
                v = s - PRING
                if v >= 0:
                    act.wait_ge(S["pved"], GB * b + len(GROUPS) * (v // UH) + group_of(v % UH) + 1)
                elif earlier(b):
                    act.wait_ge(S["pved"], GB * (b - 1) + len(GROUPS) + group_of((v + UB) % UH) + 1)
                fn(prob[:, s % PRING, 0:w], ps[:, TB + s % 2, 0:w], ACT.Exp, scale=SCALE)\
                    .then_inc(S["expd"], 1)

            def copy_sums(b, half):
                act.wait_ge(S["pved"], GB * b + len(GROUPS) * (half + 1))
                if earlier(b):
                    act.wait_ge(S["o_tr"], 2 * b + half - 1)
                fn(oS[:, half, :], ps[:, OB, :], ACT.Copy).then_inc(S["o_copied"], 1)

            def output(b, u, s):
                if s == 5:
                    copy_sums(b, 1)
                if s == 15:
                    act.wait_ge(S["oT_tr"], b + 1)
                    if earlier(b):
                        act.wait_ge(S["proj_mm"], b)
                    fn(oT[:, :], ps[:, M0, :], ACT.Copy).then_inc(S["oT_copied"], 1)
                if s in (28, 29):
                    act.wait_ge(S["s2_cen"], b + 1)
                    if earlier(b):
                        act.wait_ge(S["s2_v"], b)
                        act.wait_ge(S["s2_var"], NT * b)
                    for j in range(2 * (s - 28), 2 * (s - 28) + 2):
                        fn(l2q[:, j, :], l2[:, j, :], ACT.Square, accum_out=l2s[:, 1, j:j + 1]).then_inc(S["s2_var"], 1)
                if s in (35, 36):
                    act.wait_ge(S["s2_rstd"], b + 1)
                    for j in range(2 * (s - 35), 2 * (s - 35) + 2):
                        fn(l2[:, j, :], l2[:, j, :], ACT.Copy, scale=l2s[:, 3, j:j + 1]).then_inc(S["s2_norm"], 1)

            def route(b, u, s):
                if s == 2:
                    act.wait_ge(S["h2T_tr"], b + 1)
                    if earlier(b):
                        act.wait_ge(S["logit_mm"], b)
                    fn(h2T[:, :], ps[:, M0, :], ACT.Copy).then_inc(S["h2T_copied"], 1)
                if s == 4:
                    act.wait_ge(S["h2_b"], b + 1)
                    if earlier(b, 2):
                        act.wait_ge(S[f"scattered{b % 2}"], 16 * 2 * NT * (b // 2))
                    fn(rows[:, u, 1, :, 0:C], rows[:, u, 0, :, 0:C], ACT.Copy).then_inc(S["rows_b"], 1)
                if s == 13:
                    act.wait_ge(S["g_gap"], b + 1)
                    if earlier(b):
                        act.wait_ge(S["g_two"], b)
                    fn(gexp[:, :], gap[:, :], ACT.Exp).then_inc(S["g_exp"], 1)

            def step(t, u):
                for s in range(UB):
                    if begun(t + 2):
                        prepare(t + 2, u, s)
                    if begun(t - 1):
                        output(t - 1, 1 - u, s)
                    if begun(t - 2):
                        route(t - 2, u, s)
                    if s == 10 and begun(t):
                        copy_maxima(t, 1)
                    if s == 27 and begun(t):
                        copy_sums(t, 0)
                    if s == 32 and begun(t + 1):
                        copy_maxima(t + 1, 0)
                    if begun(t):
                        exps(t, u, s)

            timeline(act, step)

            act.wait_ge(S["g_two"], B)
            fn(gexp[:, 0:1], gexp[:, 0:1], ACT.Gelu).then_inc(S["table_in"], 1)

            def gelu(n, q, e):
                if not earlier(n):
                    act.wait_ge(S["b_in"], 32)
                if earlier(n, 2):
                    act.wait_ge(S["y_mm"], n - 1)
                for k in range(NF):
                    act.wait_ge(S["hid_mm"], NF * n + k + 1)
                    fn(hid[:, q % 2, k, :], ps[:, k, :], ACT.Gelu,
                       bias=b1_sb[:, bass.ds(NF * e + k, 1)]).then_inc(S["hid_done"], 1)

            for n in range(2 * E):
                gelu(n, n % 4, n // 2)

        @block.vector
        def _(dve):
            tt, ts, red = nc.vector.tensor_tensor, nc.vector.tensor_scalar, nc.vector.tensor_reduce
            stt, cp = nc.vector.scalar_tensor_tensor, nc.vector.tensor_copy

            def clear(z):
                nc.vector.memset(qrows[64:P, z].bitcast(U32), 0).then_inc(S[f"clear{z}"], 1)

            clear(0)
            dve.wait_ge(S["c_exp"], 1)
            ts(csig[:, :], csig[:, :], 1.0, None, ALU.add).then_inc(S["c_one"], 1)
            dve.wait_ge(S["c_one"], 1)
            nc.vector.reciprocal(csig[:, :], csig[:, :]).then_inc(S["c_rec"], 1)
            dve.wait_ge(S["c_rec"], 1)
            dve.wait_ge(S["mod_w_in"], 32)
            tt(csilu[:, :], csig[:, :], cT_sb[:, :], ALU.mult).then_inc(S["c_silu"], 1)
            dve.wait_ge(S["modT_mm"], 1)
            cp(saT[:, :], ps[:, M0, 0:B]).then_inc(S["mod_T"], 1)
            ts(caT[:, :], ps[:, M0, B:2 * B], 1.0, None, ALU.add).then_inc(S["mod_T"], 1)
            nc.vector.memset(carry[:, :], 0.0).then_inc(S["carry0"], 1)
            dve.wait_ge(S["carry0"], 1)
            dve.wait_ge(S["consts_b"], 2)

            def modulation_rows():
                dve.wait_ge(S["mod_row"], 1)
                ts(msgn, mrow, 0.0, 2.0, ALU.is_ge, ALU.mult).then_inc(S["mod_sgn"], 1)
                dve.wait_ge(S["mod_sgn"], 1)
                ts(msgn, msgn, 1.0, None, ALU.subtract).then_inc(S["mod_sgn1"], 1)
                dve.wait_ge(S["mod_sgn1"], 1)
                for n, (a, z) in enumerate(((0, C), (3 * C, 4 * C))):
                    tt(mrow[:, a:z], mrow[:, a:z], msgn[:, a:z], ALU.mult).then_inc(S["mod_abs"], 1)
                    dve.wait_ge(S["mod_abs"], n + 1)
                    ts(mrow[:, a:z], mrow[:, a:z], 0.25, None, ALU.max).then_inc(S["mod_max"], 1)
                    dve.wait_ge(S["mod_max"], n + 1)
                    tt(mrow[:, a:z], mrow[:, a:z], msgn[:, a:z], ALU.mult).then_inc(S["mod_out"], 1)
                ts(mrow[:, 2 * C:3 * C], mrow[:, 2 * C:3 * C], 1.0, None, ALU.add).then_inc(S["mod_out"], 1)

            def prepare(b, u, s):
                if s == 0:
                    if b < 2:
                        dve.wait_ge(S["x_in" if b else "x0_in"], 16)
                    if earlier(b):
                        dve.wait_ge(S["s1_cen"], b)
                    red(l1s[:, 0, :], xall[:, b], AX.X, ALU.add).then_inc(S["s1_sum"], 1)
                if s == 2:
                    dve.wait_ge(S["s1_sum"], b + 1)
                    if earlier(b):
                        dve.wait_ge(S["s1_tr"], b)
                    stt(l1[:, :, :], l1s[:, 0, :].unsqueeze(2).to_broadcast([P, NT, C]), -1.0 / C, xall[:, b],
                        ALU.mult, ALU.add).then_inc(S["s1_cen"], 1)
                for (z, z32, part, s1) in (("q", q32, qpart, 18), ("k", k32, kpart, 22)):
                    if s == s1:
                        dve.wait_ge(S[z + "1"], b + 1)
                        if earlier(b):
                            dve.wait_ge(S[z + "3"], b)
                        tt(z32[:, :], ps[:, M1, :], part[:, 0, :], ALU.subtract).then_inc(S[z + "r"], 1)

            def maximum(b, s):
                half, (kind, pos, nh) = s // UH, UNITS[s % UH]
                w = width(kind)
                dve.wait_ge(S["scored"], UB * b + s + 1)
                if s % UH == 0 and earlier(b):
                    dve.wait_ge(S["nr"], 2 * b + half - 1)
                red(negmax[:, half, NT - 1 - kind, pos:pos + nh],
                    ps[:, SB_ + sbank(s), 0:nh * w].rearrange("p (n w) -> p n w", n=nh),
                    AX.X, ALU.max, negate=True).then_inc(S["maxed"], 1)

            def split_maxima(b, half, n):
                z = 2 * b + half
                def part(i):
                    return mparts[:, half, :, i, :]
                if n == 0:
                    dve.wait_ge(S["maxed"], UB * b + UH * (half + 1))
                    if earlier(b):
                        dve.wait_ge(S["m_tr"], z - 1)
                    cp(part(0), negmax[:, half]).then_inc(S["n1"], 1)
                if n == 1:
                    dve.wait_ge(S["n1"], z + 1)
                    tt(negrest[:, half], negmax[:, half], part(0), ALU.subtract).then_inc(S["nr"], 1)
                if n == 2:
                    dve.wait_ge(S["nr"], z + 1)
                    cp(part(1), negrest[:, half]).then_inc(S["n2"], 1)
                if n == 3:
                    dve.wait_ge(S["n2"], z + 1)
                    tt(part(2), negrest[:, half], part(1), ALU.subtract).then_inc(S["n3"], 1)

            def normalise(b, half, n):
                z = 2 * b + half
                sums = ps[:, M0, :].rearrange("p (x c) -> p x c", c=32)
                if n == 0:
                    dve.wait_ge(S["o_tr"], z + 1)
                    if earlier(b):
                        dve.wait_ge(S["o_norm"], 2 * z - 2)
                    nc.vector.reciprocal(rsum[:, half], sums[:, :, D:2 * D + 2:D + 1]).then_inc(S["o_rec"], 1)
                else:
                    dve.wait_ge(S["o_rec"], z + 1)
                    if earlier(b):
                        dve.wait_ge(S["oT_tr"], b)
                    i = n - 1
                    dst = on[:, :, half * 64:half * 64 + 64].rearrange("p j (g c) -> p j g c", g=4)
                    src = sums.rearrange("p (j g) c -> p j g c", g=4)
                    rs = rsum[:, half].rearrange("p (j g) i -> p j g i", g=4)
                    tt(dst[:, :, :, D * i:D * i + D], src[:, :, :, (D + 1) * i:(D + 1) * i + D],
                       rs[:, :, :, i:i + 1].to_broadcast([P, NT, 4, D]), ALU.mult).then_inc(S["o_norm"], 1)

            def output(b, u, s):
                if s in (10, 11, 12):
                    normalise(b, 1, s - 10)
                if s == 22:
                    dve.wait_ge(S["proj_mm"], b + 1)
                    tt(xall[:, b], ps[:, M0, :].rearrange("p (j c) -> p j c", j=NT), xall[:, b], ALU.add)\
                        .then_inc(S["x1_done"], 1)
                if s == 24:
                    dve.wait_ge(S["x1_done"], b + 1)
                    if earlier(b):
                        dve.wait_ge(S["s2_cen"], b)
                    red(l2s[:, 0, :], xall[:, b], AX.X, ALU.add).then_inc(S["s2_sum"], 1)
                if s == 26:
                    dve.wait_ge(S["s2_sum"], b + 1)
                    if earlier(b):
                        dve.wait_ge(S["h2_a"], b)
                    stt(l2[:, :, :], l2s[:, 0, :].unsqueeze(2).to_broadcast([P, NT, C]), -1.0 / C, xall[:, b],
                        ALU.mult, ALU.add).then_inc(S["s2_cen"], 1)

            def over_experts(v):
                return v.unsqueeze(2).to_broadcast([P, NT, E])

            def over_tiles(v):
                return v.unsqueeze(1).to_broadcast([P, NT, E])

            def route(b, u, s):
                if s == 7:
                    dve.wait_ge(S["logit_mm"], b + 1)
                    if earlier(b):
                        dve.wait_ge(S["r_log2"], b)
                    tt(lg[:, :, :], ps[:, M0, 0:NT * E].rearrange("p (j e) -> p j e", j=NT),
                       over_tiles(br_sb[:, :]), ALU.add).then_inc(S["r_log"], 1)
                for k, (s0, src) in enumerate((((8, 8, 9, 9, 10), lg), ((11, 11, 12, 12, 13), lg2))):
                    z = str(k + 1)
                    prev = "r_log" if k == 0 else "r_log2"
                    if s == s0[0]:
                        dve.wait_ge(S[prev], b + 1)
                        if earlier(b):
                            dve.wait_ge(S["g_gap"], b)
                        red(top[:, k, :], src[:, :, :], AX.X, ALU.max).then_inc(S["r_top" + z], 1)
                    if s == s0[1]:
                        dve.wait_ge(S["r_top" + z], b + 1)
                        tt(eq[:, :, :], src[:, :, :], over_experts(top[:, k, :]), ALU.is_equal)\
                            .then_inc(S["r_eq" + z], 1)
                    if s == s0[2]:
                        dve.wait_ge(S["r_eq" + z], b + 1)
                        tt(pick[:, :, :], eq[:, :, :], over_tiles(erev[:, :]), ALU.mult).then_inc(S["r_pick" + z], 1)
                    if s == s0[3]:
                        dve.wait_ge(S["r_pick" + z], b + 1)
                        if earlier(b):
                            dve.wait_ge(S["r_swap"], b)
                        red(best[:, k], pick[:, :, :], AX.X, ALU.max).then_inc(S["r_best" + z], 1)
                    if s == s0[4]:
                        dve.wait_ge(S["r_best" + z], b + 1)
                        if earlier(b):
                            dve.wait_ge(S["r_prod2"], b)
                        tt(hot[:, k], over_tiles(erev[:, :]), over_experts(best[:, k]), ALU.is_equal)\
                            .then_inc(S["r_hot" + z], 1)
                if s == 10:
                    dve.wait_ge(S["r_hot1"], b + 1)
                    stt(lg2[:, :, :], hot[:, 0], NEG, lg[:, :, :], ALU.mult, ALU.add).then_inc(S["r_log2"], 1)
                if s == 12:
                    dve.wait_ge(S["r_top2"], b + 1)
                    if earlier(b):
                        dve.wait_ge(S["g_exp"], b)
                    tt(gap[:, :], top[:, 1, :], top[:, 0, :], ALU.subtract).then_inc(S["g_gap"], 1)
                if s == 13:
                    dve.wait_ge(S["r_hot2"], b + 1)
                    if earlier(b):
                        dve.wait_ge(S["rank_mm"], b)
                    tt(sel[:, :, :], hot[:, 0], hot[:, 1], ALU.add).then_inc(S["r_sel"], 1)
                if s == 14:
                    dve.wait_ge(S["r_best2"], b + 1)
                    if earlier(b):
                        dve.wait_ge(S["id_set"], 2 * b)
                    tt(swap[:, :], best[:, 1, :], best[:, 0, :], ALU.is_gt).then_inc(S["r_swap"], 1)
                if s == 15:
                    dve.wait_ge(S["r_swap"], b + 1)
                    dve.wait_ge(S["id_next"], b + 1)
                    if earlier(b, 2):
                        dve.wait_ge(S[f"scattered{b % 2}"], 16 * 2 * NT * (b // 2))
                    for k in range(2):
                        stt(rows[:, u, k, :, C + 1], swap[:, :], float(N - 2 * N * k), tokid[:, k, :],
                            ALU.mult, ALU.add).then_inc(S["id_set"], 1)
                if s == 15:
                    dve.wait_ge(S["g_exp"], b + 1)
                    ts(gden[:, :], gexp[:, :], 1.0, None, ALU.add).then_inc(S["g_den"], 1)
                if s == 16:
                    dve.wait_ge(S["g_den"], b + 1)
                    if earlier(b, 2):
                        dve.wait_ge(S[f"scattered{b % 2}"], 16 * 2 * NT * (b // 2))
                    nc.vector.reciprocal(rows[:, u, 0, :, C], gden[:, :]).then_inc(S["g_one"], 1)
                if s == 17:
                    dve.wait_ge(S["g_one"], b + 1)
                    tt(rows[:, u, 1, :, C], gexp[:, :], rows[:, u, 0, :, C], ALU.mult).then_inc(S["g_two"], 1)
                if s == 18:
                    dve.wait_ge(S["rank_mm"], b + 1)
                    if earlier(b):
                        dve.wait_ge(S["r_prod"], b)
                        dve.wait_ge(S["r_carry"], b)
                    tt(rank[:, :, :], ps[:, M0, 0:NT * E].rearrange("p (j e) -> p j e", j=NT),
                       over_tiles(carry[:, :]), ALU.add).then_inc(S["r_rank"], 1)
                    dve.wait_ge(S["r_rank"], b + 1)
                    tt(carry[:, :], ps[:, M0, NT * E:(NT + 1) * E], carry[:, :], ALU.add)\
                        .then_inc(S["r_carry"], 1)
                if s == 19:
                    dve.wait_ge(S["r_rank"], b + 1)
                    if earlier(b):
                        dve.wait_ge(S["r_prod2"], b)
                    tt(slot[:, :, :], rank[:, :, :], over_tiles(eoff[:, :]), ALU.add).then_inc(S["r_slot"], 1)
                if s == 19:
                    if earlier(b):
                        dve.wait_ge(S["r_myrank"], b)
                        dve.wait_ge(S["r_myslot"], b)
                    dve.wait_ge(S["r_hot2"], b + 1)
                    for k in range(2):
                        last = tt(prod[:, k], hot[:, k], rank[:, :, :], ALU.mult)
                    last.then_inc(S["r_prod"], 1)
                if s == 20:
                    dve.wait_ge(S["r_slot"], b + 1)
                    for k in range(2):
                        last = tt(prod2[:, k], hot[:, k], slot[:, :, :], ALU.mult)
                    last.then_inc(S["r_prod2"], 1)
                if s == 21:
                    dve.wait_ge(S["r_prod"], b + 1)
                    if earlier(b):
                        dve.wait_ge(S["r_over"], b)
                    red(myrank[:, :, :], prod[:, :, :, :], AX.X, ALU.add).then_inc(S["r_myrank"], 1)
                if s == 22:
                    dve.wait_ge(S["r_prod2"], b + 1)
                    if earlier(b):
                        dve.wait_ge(S["r_index"], b)
                    red(myslot[:, :, :], prod2[:, :, :, :], AX.X, ALU.add).then_inc(S["r_myslot"], 1)
                if s == 23:
                    dve.wait_ge(S["r_myrank"], b + 1)
                    ts(over[:, :, :], myrank[:, :, :], float(CAP), FAR, ALU.is_ge, ALU.mult).then_inc(S["r_over"], 1)
                if s == 24:
                    dve.wait_ge(S["r_over"], b + 1)
                    dve.wait_ge(S["r_myslot"], b + 1)
                    if earlier(b, 2):
                        dve.wait_ge(S[f"scattered{b % 2}"], 16 * 2 * NT * (b // 2))
                    tt(index[:, u], myslot[:, :, :], over[:, :, :], ALU.add).then_inc(S["r_index"], 1)

            def step(t, u):
                for s in range(UB):
                    if t == -2 and s == 4:
                        modulation_rows()
                    if t == -2 and s == 26:
                        clear(1)
                    if s < 4 and begun(t):
                        split_maxima(t, 1, s)
                    if 23 <= s < 27 and begun(t + 1):
                        split_maxima(t + 1, 0, s - 23)
                    if begun(t + 2):
                        prepare(t + 2, u, s)
                    if begun(t - 2):
                        route(t - 2, u, s)
                    if begun(t - 1):
                        output(t - 1, 1 - u, s)
                    if s in (32, 33, 35) and begun(t):
                        normalise(t, 0, (32, 33, 35).index(s))
                    if begun(t + 1):
                        maximum(t + 1, s)

            timeline(dve, step)

            def slots_copy(n, q, e):
                dve.wait_ge(S["slot_tr"], n + 1)
                if earlier(n, 2):
                    dve.wait_ge(S["hid_mm"], NF * (n - 1))
                cp(slotT[:, q % 2, :], ps[:, 6, :]).then_inc(S["slot_T"], 1)
                if earlier(n, 4):
                    dve.wait_ge(S[f"picked{q % 2}"], 16 * NT * (e - 1))
                    dve.wait_ge(S["y_done"], n - 3)
                cp(gate[:, q, :], slotin[:, q % 2, :, C]).then_inc(S["gate_done"], 1)
                cp(dest[:, q, :], slotin[:, q % 2, :, C + 1]).then_inc(S["dest_done"], 1)

            def finish(n, q, e):
                dve.wait_ge(S["y_mm"], n + 1)
                if earlier(n):
                    dve.wait_ge(S["y_done"], n)
                tt(ysum, ps[:, 4 + q % 2, :].rearrange("p (j c) -> p j c", j=NT),
                   b2_sb[:, bass.ds(e, 1), :].to_broadcast([P, NT, C]), ALU.add).then_inc(S["y_add"], 1)
                dve.wait_ge(S["y_add"], n + 1)
                dve.wait_ge(S["gate_done"], n + 1)
                if earlier(n, 2):
                    dve.wait_ge(S[f"picked{q % 2}"], 16 * NT * e)
                tt(yout[:, q % 2], ysum, gate[:, q, :].unsqueeze(2).to_broadcast([P, NT, C]), ALU.mult)\
                    .then_inc(S["y_done"], 1)

            dve.wait_ge(S["b_in"], 32)
            slots_copy(0, 0, 0)
            slots_copy(1, 1, 0)
            for n in range(4):
                slots_copy(n + 2, (n + 2) % 4, (n + 2) // 2)
                finish(n, n, n // 2)
            with dve.Fori(1, E // 2 - 1) as i:
                for q in range(4):
                    slots_copy(4 * i + q + 2, (q + 2) % 4, 2 * i + (q + 2) // 2)
                    finish(4 * i + q, q, 2 * i + q // 2)
            def scale(b, k):
                if k:
                    dve.wait_ge(two_in[b], 16)
                elif b % 4 == 0:
                    dve.wait_ge(low_in[b // 4], 16 * 4)
                tt(two[:, b, k], two[:, b, k], modB[:, b:b + 1, 3 * C:4 * C].to_broadcast([P, NT, C]),
                   ALU.mult).then_inc(S["two_gb"], 1)

            def add(b, k):
                dve.wait_ge(S["two_gb"], B * k + b + 1)
                if k:
                    dve.wait_ge(S["x2_even"], b // 2 + 1)
                tt(xall[:, b], xall[:, b], two[:, b, k], ALU.add).then_inc(S["x2_even"], 1)

            for n in range(2 * E - 4, 2 * E):
                if n + 2 < 2 * E:
                    slots_copy(n + 2, (n + 2) % 4, (n + 2) // 2)
                finish(n, n % 4, n // 2)

            for k in range(2):
                for b in range(B):
                    scale(b, k)
                    if b % 2:
                        add(b - 1, k)

        @block.gpsimd
        def _(pool):
            sel_, tt, ts = nc.gpsimd.affine_select, nc.gpsimd.tensor_tensor, nc.gpsimd.tensor_scalar
            ms = nc.gpsimd.memset
            ms(ident[:, :], 0.0).then_inc(S["ident0"], 1)
            ms(identb[:, :], 0.0).then_inc(S["ident0"], 1)
            ms(mask[:, :, :], 0.0).then_inc(S["ident0"], 1)
            ms(upper[:, :], 1.0).then_inc(S["ident0"], 1)
            ms(empty[:, :], 0.0).then_inc(S["ident0"], 1)
            ms(onesb[:, :], 1.0).then_inc(S["consts"], 1)
            ms(vhalf[:, :], -0.5).then_inc(S["consts"], 1)
            ms(zeros[:, :], 0.0).then_inc(S["consts"], 1)
            pool.wait_ge(S["ident0"], 5)
            ms(empty[:, C + 1:C + 2], FAR).then_inc(S["consts"], 1)
            sel_(out=ident[:, :], in_=ident[:, :], compare_op=ALU.not_equal, fill=1.0, base=0,
                 pattern=[[-1, P]], channel_multiplier=1).then_inc(S["consts"], 1)
            sel_(out=identb[:, :], in_=identb[:, :], compare_op=ALU.not_equal, fill=1.0, base=0,
                 pattern=[[-1, P]], channel_multiplier=1).then_inc(S["consts"], 1)
            sel_(out=mask[:, :, :], in_=mask[:, :, :], compare_op=ALU.is_ge, fill=NEG, base=0,
                 pattern=[[0, 4], [-1, P]], channel_multiplier=1).then_inc(S["consts"], 1)
            sel_(out=upper[:, :], in_=upper[:, :], compare_op=ALU.is_gt, fill=0.0, base=0,
                 pattern=[[1, P]], channel_multiplier=-1).then_inc(S["consts"], 1)
            nc.gpsimd.iota(erev[:, :], [[-1, E]], base=E, channel_multiplier=0,
                           allow_small_or_imprecise_dtypes=True).then_inc(S["consts_b"], 1)
            nc.gpsimd.iota(eoff[:, :], [[CAP, E]], base=0, channel_multiplier=0,
                           allow_small_or_imprecise_dtypes=True).then_inc(S["consts_b"], 1)
            nc.gpsimd.iota(tokid[:, :, :], [[N, 2], [P, NT]], base=0, channel_multiplier=1,
                           allow_small_or_imprecise_dtypes=True).then_inc(S["id_next"], 1)

            def clear(z):
                ms(krows[:, z].bitcast(U32), 0).then_inc(S[f"clear{z}"], 1)

            def clear_values():
                ms(vpad[:, :, :, :, :], 0.0).then_inc(S["vclear"], 1)
                pool.wait_ge(S["vclear"], 1)
                vslot = vpad[:, :, :, :, :].rearrange("p a j (x i) c -> p (a j x) i c", i=2)
                for i in range(2):
                    ms(vslot[:, :, i, (D + 1) * i + D], 1.0).then_inc(S["vones"], 1)

            def prepare(b, u, s):
                if s == 6:
                    pool.wait_ge(S["s1_var"], NT * (b + 1))
                    ts(l1s[:, 2, :], l1s[:, 1, :], 1.0 / C, EPS, ALU.mult, ALU.add).then_inc(S["s1_v"], 1)
                if s == 7:
                    pool.wait_ge(S["s1_v"], b + 1)
                    if earlier(b):
                        pool.wait_ge(S["s1_norm"], NT * b)
                    tt(l1s[:, 3, :], l1s[:, 2, :], vhalf[:, :], ALU.pow).then_inc(S["s1_rstd"], 1)
                for (z, z32, part, s3) in (("q", q32, qpart, 21), ("k", k32, kpart, 25)):
                    if s == s3:
                        pool.wait_ge(S[z + "2"], b + 1)
                        if earlier(b):
                            pool.wait_ge(S["qk_stored"], 48 * b)
                        tt(part[:, 2, :], z32[:, :], part[:, 1, :], ALU.subtract).then_inc(S[z + "3"], 1)

            def gate_projection(b):
                if earlier(b):
                    pool.wait_ge(S["proj_mm"], b)
                else:
                    pool.wait_ge(S["wo_in"], 16)
                    pool.wait_ge(S["modB_in"], 16)
                tt(wo_ga[:, :], wo_sb[:, :], modB[:, b, 0:C], ALU.mult).then_inc(S["wo_ga"], 1)

            def place_values(b, par):
                if not earlier(b):
                    pool.wait_ge(S["vones"], 2)
                pool.wait_ge(S["v_copied"], b + 1)
                if earlier(b, 2):
                    pool.wait_ge(S["pved"], GB * (b - 1))
                dst = vpad[:, par].rearrange("p j (x i) c -> p (j x) i c", i=2)
                src = vtmp[:, :, :].rearrange("p j (x i d) -> p (j x) i d", i=2, d=D)
                for i in range(2):
                    last = nc.gpsimd.tensor_copy(dst[:, :, i, (D + 1) * i:(D + 1) * i + D], src[:, :, i, :])
                last.then_inc(S["v_placed"], 1)

            def causal(b, s):
                kind, pos, nh = UNITS[s % UH]
                w = width(kind)
                pool.wait_ge(S["expd"], UB * b + s + 1)
                blk = prob[:, s % PRING, 0:nh * w].rearrange("p (n w) -> p n w", n=nh)[:, :, 0:P]
                sel_(out=blk, in_=blk, compare_op=ALU.is_ge, fill=0.0, base=0,
                     pattern=[[0, nh], [1, P]], channel_multiplier=-1).then_inc(S["masked"], 1)

            def output(b, u, s):
                if s == 30:
                    pool.wait_ge(S["s2_var"], NT * (b + 1))
                    ts(l2s[:, 2, :], l2s[:, 1, :], 1.0 / C, EPS, ALU.mult, ALU.add).then_inc(S["s2_v"], 1)
                if s == 31:
                    pool.wait_ge(S["s2_v"], b + 1)
                    if earlier(b):
                        pool.wait_ge(S["s2_norm"], NT * b)
                    tt(l2s[:, 3, :], l2s[:, 2, :], vhalf[:, :], ALU.pow).then_inc(S["s2_rstd"], 1)
                if s == 37:
                    pool.wait_ge(S["s2_norm"], NT * (b + 1))
                    if earlier(b):
                        pool.wait_ge(S["h2_b"], b)
                    tt(h2[:, :, :], l2[:, :, :], modB[:, bass.ds(b, 1), 2 * C:3 * C].to_broadcast([P, NT, C]),
                       ALU.mult).then_inc(S["h2_a"], 1)
                if s == 39:
                    pool.wait_ge(S["h2_a"], b + 1)
                    if earlier(b, 2):
                        pool.wait_ge(S[f"scattered{b % 2}"], 16 * 2 * NT * (b // 2))
                        pool.wait_ge(S["h2T_tr"], b)
                        pool.wait_ge(S["rows_b"], b)
                    tt(rows[:, u, 0, :, 0:C], h2[:, :, :],
                       modB[:, bass.ds(b, 1), C:2 * C].to_broadcast([P, NT, C]), ALU.add).then_inc(S["h2_b"], 1)

            def route(b, u, s):
                if s == 18:
                    pool.wait_ge(S["id_set"], 2 * (b + 1))
                    ts(tokid[:, :, :], tokid[:, :, :], float(T), None, ALU.add).then_inc(S["id_next"], 1)
                if s == 26:
                    pool.wait_ge(S["r_index"], b + 1)
                    pool.wait_ge(S["g_two"], b + 1)
                    pool.wait_ge(S["rows_b"], b + 1)
                    pool.wait_ge(S["prefilled"], 32)

            def scatter(b, u, n):
                k, j = divmod(n, NT)
                if n == 0:
                    pool.wait_ge(S["id_set"], 2 * (b + 1))
                pool.indirect_dma_start(slots, bass.IndirectOffsetOnAxis(index[:, u, k, j:j + 1], 0),
                                        rows[:, u, k, j, :], None, bounds_check=E * CAP - 1,
                                        oob_is_err=False).then_inc(S[f"scattered{b % 2}"], 16)

            def step(t, u):
                for s in range(UB):
                    if t == -2 and s == 26:
                        clear(1)
                    if s == 4 and begun(t + 1):
                        place_values(t + 1, 1 - u)
                    if s == 24 and begun(t):
                        gate_projection(t)
                    if begun(t + 2):
                        prepare(t + 2, u, s)
                    if begun(t - 1):
                        output(t - 1, 1 - u, s)
                    if begun(t - 2):
                        route(t - 2, u, s)
                    if begun(t):
                        causal(t, s)
                    for n in range(2 * NT):
                        if t < B:
                            if s == 4 * n + 26 and begun(t - 2):
                                scatter(t - 2, u, n)
                        elif s == 41:
                            scatter(t - 2, u, n)
                        if s == 4 * n - 18 and begun(t - 3) and t <= B:
                            scatter(t - 3, 1 - u, n)

            clear(0)
            clear_values()
            timeline(pool, step)

            def send(n, q):
                pool.wait_ge(S["y_done"], n + 1)
                for j in range(NT):
                    pool.indirect_dma_start(picks, bass.IndirectOffsetOnAxis(dest[:, q, j:j + 1], 0),
                                            yout[:, q % 2, j, :], None, bounds_check=2 * N - 1,
                                            oob_is_err=False).then_inc(S[f"picked{q % 2}"], 16)

            for n in range(2 * E):
                send(n, n % 4)

            for k in range(2):
                for b in range(1, B, 2):
                    pool.wait_ge(S["two_gb"], B * k + b + 1)
                    if k:
                        pool.wait_ge(S["x2_odd"], b // 2 + 1)
                    tt(xall[:, b], xall[:, b], two[:, b, k], ALU.add).then_inc(S["x2_odd"], 1)


def kernel(L0_attn_x, L0_attn_Q, L0_attn_K, L0_attn_V, L0_attn_O, L0_ffn_Wr, L0_ffn_br, L0_ffn_W1,
           L0_ffn_b1, L0_ffn_W2, L0_ffn_b2, L0_c, L0_wmod):
    import numpy as np
    import concourse.bacc as bacc
    from concourse.bass_utils import run_bass_kernel_spmd

    heads = [half * HH + h for half in range(HALVES) for h in ORDER]

    def by_position(w):
        return np.asarray(w)[:, heads, :].transpose(0, 2, 1).reshape(C, C)

    arrays = {
        "x": L0_attn_x,
        "wq": by_position(L0_attn_Q),
        "wk": by_position(L0_attn_K),
        "wv": np.asarray(L0_attn_V).reshape(C, C),
        "wo": L0_attn_O,
        "wr": L0_ffn_Wr,
        "br": L0_ffn_br,
        "w1": L0_ffn_W1,
        "b1": np.asarray(L0_ffn_b1).reshape(E * NF, P).transpose(1, 0),
        "w2": L0_ffn_W2,
        "b2": L0_ffn_b2,
        "cT": np.asarray(L0_c).transpose(1, 0),
        "wmod": L0_wmod,
    }
    arrays = {"in_" + n: np.ascontiguousarray(a) for n, a in arrays.items()}
    nc = bacc.Bacc("TRN2", target_bir_lowering=False, num_devices=1)
    aps = [nc.dram_tensor(n, a.shape, mybir.dt.from_np(a.dtype), kind="ExternalInput").ap()
           for n, a in arrays.items()]
    out = nc.dram_tensor("out_0", (B, T, C), F32, kind="ExternalOutput").ap()
    adaln_moe_kernel(nc, *aps, out)
    r = run_bass_kernel_spmd(nc, [arrays], core_ids=[0])
    return r.results[0]["out_0"]
```
